# Optimizing a Trainium2 kernel written in Bass

```python
import numpy as np
import jax
import jax.numpy as jnp

def _softmax(x, axis=-1):
    return jax.nn.softmax(x, axis=axis)

def _gelu(x):
    return jax.nn.gelu(x, approximate=True)

def _silu(x):
    return jax.nn.silu(x)

def _sigmoid(x):
    return jax.nn.sigmoid(x)

def _layernorm(x, axis=-1, eps=1e-05):
    m = jnp.mean(x, axis=axis, keepdims=True)
    v = jnp.var(x, axis=axis, keepdims=True)
    return (x - m) / jnp.sqrt(v + eps)

def _scatter_add(tgt, idx, src, axis=0):
    return tgt.at[idx].add(src)

def _segment_sum(src, seg, n):
    return jax.ops.segment_sum(src, seg, n)
kernel_name = 'mk_xattn_ffn_d1_seqx_r8_48dec6'

def setup_inputs(seed: int=0):
    np.random.seed(seed)
    _w = jnp.asarray

    def _rec_inputs():
        import jax
        import jax.numpy as jnp
        _rk = jax.random.key(seed)
        x = 7.22e-05 + 1 * jax.random.normal(jax.random.fold_in(_rk, 1), (64, 64, 128), jnp.float32)
        _lenS = 64 - jax.random.randint(jax.random.fold_in(_rk, 7), (64,), 0, max(1, 64 // 4) + 1, jnp.int32)
        _lenS2 = 64 - jax.random.randint(jax.random.fold_in(_rk, 8), (64,), 0, max(1, 64 // 4) + 1, jnp.int32)
        _ctx_1024P = jax.random.normal(jax.random.fold_in(_rk, 11), (64, 16, 128), jnp.float32)
        _ctx_1024c = jax.random.dirichlet(jax.random.fold_in(_rk, 511), 0.3 * jnp.ones((16,), jnp.float32), (64, 64))
        _ctx_1024t = jnp.einsum('bsk,bkd->bsd', _ctx_1024c, _ctx_1024P)
        _ctx_1024t = _ctx_1024t * jax.lax.rsqrt(jnp.mean(jnp.square(_ctx_1024t)) + 1e-12) * 0.953939
        ctx_1024 = 4.13588e-05 + 0.999923 * (_ctx_1024t + 0.3 * jax.random.normal(jax.random.fold_in(_rk, 611), (64, 64, 128), jnp.float32))
        return (x, ctx_1024)
    x, ctx_1024 = _rec_inputs()

    def _L0_xattn_setup():
        import jax, jax.numpy as jnp
        import numpy as np
        D_MODEL = 128
        NHEAD = 16
        HEAD_DIM = D_MODEL // NHEAD
        key = jax.random.key(seed)
        ks = jax.random.split(key, 11)
        B, S, D = (4, 256, D_MODEL)
        scale = 1.0 / np.sqrt(D)
        inp = {'q': jax.random.normal(ks[0], (B, S, D), jnp.float32), 'k': jax.random.normal(ks[1], (B, S, D), jnp.float32), 'v': jax.random.normal(ks[2], (B, S, D), jnp.float32), 'Wq': jax.random.normal(ks[3], (D, D), jnp.float32) * scale, 'bq': jnp.zeros((D,), jnp.float32), 'Wk': jax.random.normal(ks[4], (D, D), jnp.float32) * scale, 'bk': jnp.zeros((D,), jnp.float32), 'Wv': jax.random.normal(ks[5], (D, D), jnp.float32) * scale, 'bv': jnp.zeros((D,), jnp.float32), 'Wo': jax.random.normal(ks[6], (D, D), jnp.float32) * scale, 'bo': jnp.zeros((D,), jnp.float32)}
        return inp
    _L0_xattn_all = _L0_xattn_setup()
    _L0_xattn_in = {k: v for k, v in _L0_xattn_all.items() if k in ('Wq', 'bq', 'Wk', 'bk', 'Wv', 'bv', 'Wo', 'bo')}
    del _L0_xattn_all

    def _L0_ffn_setup():
        import jax, jax.numpy as jnp
        import numpy as np
        B, S, H, F, E, K = (4, 256, 128, 448, 8, 2)
        CAP_FACTOR = 1.25

        def _moe_forward(hidden_states, gate_w, w1, w2, w3):
            b, s, h = hidden_states.shape
            dtype = hidden_states.dtype
            x = hidden_states.reshape(-1, h)
            router_logits = x @ gate_w.T
            expert_weights = jax.nn.softmax(router_logits.astype(jnp.float32), axis=1)
            _, selected_experts = jax.lax.top_k(expert_weights, K)
            top_k_idx = selected_experts.reshape(b, s, K)
            probs = expert_weights.reshape(b, s, E)
            capacity = int(s * K / E * CAP_FACTOR)
            expert_mask = jax.nn.one_hot(top_k_idx, E, dtype=jnp.int32)
            mask_fused = expert_mask.reshape(b, s * K, E)
            count_fused = jnp.cumsum(mask_fused, axis=1)
            count = count_fused.reshape(b, s, K, E)
            trunc_mask = expert_mask * (count <= capacity).astype(jnp.int32)
            combined_mask = trunc_mask.sum(axis=2)
            masked_probs = probs * combined_mask
            pos_fused = mask_fused * count_fused
            pos = pos_fused.reshape(b, s, K, E)
            combined_pos = pos.sum(axis=2) * combined_mask
            pos_in_cap = jax.nn.one_hot(combined_pos, capacity + 1, dtype=jnp.int32)
            combine_mask = masked_probs[..., None] * pos_in_cap
            combine_mask = combine_mask[..., 1:].astype(dtype)
            dispatch_mask = (combine_mask != 0).astype(dtype)
            dispatch = jnp.einsum('bsm,bsec->ebcm', hidden_states, dispatch_mask)
            h1 = jnp.einsum('ebcm,emh->ebch', dispatch, w1)
            h3 = jnp.einsum('ebcm,emh->ebch', dispatch, w3)
            expert_out = jnp.einsum('ebch,ehm->ebcm', jax.nn.silu(h1) * h3, w2)
            final = jnp.einsum('ebcm,bsec->bsm', expert_out, combine_mask)
            return final
        key = jax.random.key(seed)
        k1, k2, k3, k4, k5 = jax.random.split(key, 5)
        s_h = 1.0 / np.sqrt(H)
        s_f = 1.0 / np.sqrt(F)
        return {'hidden_states': jax.random.normal(k1, (B, S, H), dtype=jnp.float32), 'gate_w': jax.random.normal(k2, (E, H), dtype=jnp.float32) * s_h, 'w1': jax.random.normal(k3, (E, H, F), dtype=jnp.float32) * s_h, 'w2': jax.random.normal(k4, (E, F, H), dtype=jnp.float32) * s_f, 'w3': jax.random.normal(k5, (E, H, F), dtype=jnp.float32) * s_h}
    _L0_ffn_all = _L0_ffn_setup()
    _L0_ffn_in = {k: v for k, v in _L0_ffn_all.items() if k in ('gate_w', 'w1', 'w2', 'w3')}
    del _L0_ffn_all
    return {'x': x, 'ctx_1024': ctx_1024, 'L0_xattn_Wq': _L0_xattn_in['Wq'], 'L0_xattn_bq': _L0_xattn_in['bq'], 'L0_xattn_Wk': _L0_xattn_in['Wk'], 'L0_xattn_bk': _L0_xattn_in['bk'], 'L0_xattn_Wv': _L0_xattn_in['Wv'], 'L0_xattn_bv': _L0_xattn_in['bv'], 'L0_xattn_Wo': _L0_xattn_in['Wo'], 'L0_xattn_bo': _L0_xattn_in['bo'], 'L0_ffn_gate_w': _L0_ffn_in['gate_w'], 'L0_ffn_w1': _L0_ffn_in['w1'], 'L0_ffn_w2': _L0_ffn_in['w2'], 'L0_ffn_w3': _L0_ffn_in['w3']}

def reference(x, ctx_1024, L0_xattn_Wq, L0_xattn_bq, L0_xattn_Wk, L0_xattn_bk, L0_xattn_Wv, L0_xattn_bv, L0_xattn_Wo, L0_xattn_bo, L0_ffn_gate_w, L0_ffn_w1, L0_ffn_w2, L0_ffn_w3):
    import jax
    import jax.numpy as jnp

    def _L0_xattn_ref(q, k, v, Wq, bq, Wk, bk, Wv, bv, Wo, bo):
        import jax, jax.numpy as jnp
        import numpy as np
        D_MODEL = 128
        NHEAD = 16
        HEAD_DIM = D_MODEL // NHEAD
        B, S, D = q.shape
        H, Hd = (NHEAD, HEAD_DIM)
        qh = (q @ Wq.T + bq).reshape(B, S, H, Hd).transpose(0, 2, 1, 3)
        kh = (k @ Wk.T + bk).reshape(B, S, H, Hd).transpose(0, 2, 1, 3)
        vh = (v @ Wv.T + bv).reshape(B, S, H, Hd).transpose(0, 2, 1, 3)
        scores = jnp.einsum('bhqd,bhkd->bhqk', qh, kh) / jnp.sqrt(jnp.float32(Hd))
        attn = jax.nn.softmax(scores, axis=-1)
        out = jnp.einsum('bhqk,bhkd->bhqd', attn, vh)
        out = out.transpose(0, 2, 1, 3).reshape(B, S, D)
        return out @ Wo.T + bo

    def _L0_ffn_ref(hidden_states, gate_w, w1, w2, w3):
        import jax, jax.numpy as jnp
        import numpy as np
        B, S, H, F, E, K = (4, 256, 128, 448, 8, 2)
        CAP_FACTOR = 1.25

        def _moe_forward(hidden_states, gate_w, w1, w2, w3):
            b, s, h = hidden_states.shape
            dtype = hidden_states.dtype
            x = hidden_states.reshape(-1, h)
            router_logits = x @ gate_w.T
            expert_weights = jax.nn.softmax(router_logits.astype(jnp.float32), axis=1)
            _, selected_experts = jax.lax.top_k(expert_weights, K)
            top_k_idx = selected_experts.reshape(b, s, K)
            probs = expert_weights.reshape(b, s, E)
            capacity = int(s * K / E * CAP_FACTOR)
            expert_mask = jax.nn.one_hot(top_k_idx, E, dtype=jnp.int32)
            mask_fused = expert_mask.reshape(b, s * K, E)
            count_fused = jnp.cumsum(mask_fused, axis=1)
            count = count_fused.reshape(b, s, K, E)
            trunc_mask = expert_mask * (count <= capacity).astype(jnp.int32)
            combined_mask = trunc_mask.sum(axis=2)
            masked_probs = probs * combined_mask
            pos_fused = mask_fused * count_fused
            pos = pos_fused.reshape(b, s, K, E)
            combined_pos = pos.sum(axis=2) * combined_mask
            pos_in_cap = jax.nn.one_hot(combined_pos, capacity + 1, dtype=jnp.int32)
            combine_mask = masked_probs[..., None] * pos_in_cap
            combine_mask = combine_mask[..., 1:].astype(dtype)
            dispatch_mask = (combine_mask != 0).astype(dtype)
            dispatch = jnp.einsum('bsm,bsec->ebcm', hidden_states, dispatch_mask)
            h1 = jnp.einsum('ebcm,emh->ebch', dispatch, w1)
            h3 = jnp.einsum('ebcm,emh->ebch', dispatch, w3)
            expert_out = jnp.einsum('ebch,ehm->ebcm', jax.nn.silu(h1) * h3, w2)
            final = jnp.einsum('ebcm,bsec->bsm', expert_out, combine_mask)
            return final
        return _moe_forward(hidden_states, gate_w, w1, w2, w3)
    x = x + _L0_xattn_ref(_layernorm(x, axis=-1), ctx_1024, ctx_1024, L0_xattn_Wq, L0_xattn_bq, L0_xattn_Wk, L0_xattn_bk, L0_xattn_Wv, L0_xattn_bv, L0_xattn_Wo, L0_xattn_bo)
    x = x + _L0_ffn_ref(_layernorm(x, axis=-1), L0_ffn_gate_w, L0_ffn_w1, L0_ffn_w2, L0_ffn_w3)
    return x

_drawn_inputs = setup_inputs


def setup_inputs(seed=0):
    import zlib

    import numpy as np

    out = dict(_drawn_inputs(seed))
    spreads = {'L0_xattn_bq': (0.0, 0.1),
     'L0_xattn_bk': (0.0, 0.1),
     'L0_xattn_bv': (0.0, 0.1),
     'L0_xattn_bo': (0.0, 0.1)}
    factors = {}
    for name, (base, spread) in spreads.items():
        noise = np.random.default_rng([zlib.crc32(name.encode()), seed]).standard_normal(out[name].shape)
        drawn = base * np.exp(spread * noise) if base else spread * noise
        out[name] = jnp.asarray(drawn.astype(out[name].dtype))
    for name, factor in factors.items():
        out[name] = (out[name] * factor).astype(out[name].dtype)
    return out
```

```python
from contextlib import ExitStack

import numpy as np

import concourse.bass as bass
from concourse import mybir

ALU = mybir.AluOpType
ACT = mybir.ActivationFunctionType
F32 = mybir.dt.float32
F32R = mybir.dt.float32r
X = mybir.AxisListType.X

SEQS, SEQ, D = 64, 64, 128
HEADS = 16
HEAD = D // HEADS
EXPERTS, TOPK, FFN = 8, 2, 448
CAP = int(SEQ * TOPK / EXPERTS * 1.25)
EPS = 1e-5

P = 128
TOKENS = SEQS * SEQ
TILES = TOKENS // P
MACROS = TILES // 4
UNITS = TILES // 2
MT = 4 * P
GROUPS = 2
GH = HEADS // GROUPS
VT = HEADS // 4
VC = 4 * HEAD + 2
SLOTS = EXPERTS * CAP
HALF = SLOTS // 2
ESLOTS = SEQS * CAP
PARTS = 4
PS = ESLOTS // PARTS
CHUNKS = 4
FC = FFN // CHUNKS
CONST_COLS = dict(ident=P, tri=P, headmask=GH, place=CAP, rank=EXPERTS)


def constants():
    p = np.arange(P)
    parts = dict(
        ident=np.eye(P),
        tri=(p[:, None] // SEQ == p[None, :] // SEQ) & (p[:, None] <= p[None, :]),
        headmask=(p[:, None] % (GH * HEAD)) // HEAD == np.arange(GH)[None, :],
        place=np.tile(np.arange(1, CAP + 1), (P, 1)),
        rank=np.tile(np.arange(EXPERTS, 0, -1), (P, 1)),
    )
    return np.concatenate([np.asarray(parts[n], np.float32) for n in CONST_COLS], axis=1)


def used(eng, semaphore, count):
    if not isinstance(count, int) or count > 0:
        eng.wait_ge(semaphore, count)


def steps(eng, n, stages):
    depth = max(lag for lag, _ in stages)
    head = (depth + 3) // 2

    def slot(pair, u):
        for lag, stage in stages:
            parity = (u - lag) % 2
            half = pair + (u - lag - parity) // 2
            if isinstance(pair, int) and not 0 <= 2 * half + parity < n:
                continue
            stage(half, parity)

    for pair in range(min(head, n // 2)):
        slot(pair, 0)
        slot(pair, 1)
    if head < n // 2:
        with eng.Fori(head, n // 2) as pair:
            slot(pair, 0)
            slot(pair, 1)
    for t in range(n, n + depth):
        slot(t // 2, t % 2)


def build(nc, x, ctx_t, consts, wq, wk, wv, wo, bq, bk, bv, bo, gate, w1, w2, w3, out_t):
    with ExitStack() as stack:
        sem_names = {}

        def sem(name):
            sem_names[name] = stack.enter_context(nc.semaphore(name))
            return sem_names[name]

        ARENA = 212000
        arena = -(-nc.sbuf_base // 64) * 64
        stack.enter_context(nc.sbuf_tensor("arena", [P, ARENA], mybir.dt.uint8, align_bytes=64))
        top = {}

        def place(region, name, shape, dtype=F32):
            at = top.get(region, region)
            size = 4 * int(np.prod(shape[1:]))
            top[region] = at + size
            assert at + size <= ARENA, name
            at += -at % 32
            top[region] = at + size
            return nc.alloc_sbuf_tensor_at(name, shape, dtype, offset=arena + at)

        A = 0
        q_all = place(A, "q_all", [P, TOKENS])
        k_all = place(A, "k_all", [P, TOKENS])
        v_diag = place(A, "v_diag", [P, SEQS * VT * VC])
        x_all = place(A, "x_all", [P, TILES, D])
        A2 = 1
        top[A2] = 0
        slots_hi = place(A2, "slots_hi", [P, EXPERTS * ESLOTS], F32R)
        slots_lo = place(A2, "slots_lo", [P, EXPERTS * ESLOTS], F32R)
        A3 = 2
        top[A3] = 0
        expert_out = place(A3, "expert_out", [P, EXPERTS * ESLOTS])
        comb_in = place(A3, "comb_in", [P, 2, 8, EXPERTS, CAP])
        res_in = place(A3, "res_in", [P, 2, 4, D])
        slot_rows = place(A3, "slot_rows", [P, 16, D])
        out_ring = place(A3, "out_ring", [P, 2, MT])
        A4 = 3
        top[A4] = 0
        h_ring = place(A4, "h_ring", [P, 2, 4, D])
        ht_ring = place(A4, "ht_ring", [P, 2, MT])
        logits = place(A4, "logits", [P, TILES, EXPERTS])
        rt = [place(A4, f"route_{i}", [P, TILES, EXPERTS]) for i in range(8)]
        rs = [place(A4, f"route_s{i}", [P, TILES]) for i in range(6)]

        B = 83968
        x1_all = place(B, "x1_all", [P, TILES, D])
        C = B + 16384
        comb_t = place(C, "comb_t", [P, 2, TOKENS])
        C2 = C + 1
        top[C2] = C
        q_diag = place(C2, "q_diag", [P, 2, 2, GH, SEQ])
        k_ring = place(C2, "k_ring", [P, 2, P])
        probs = place(C2, "probs", [P, 2, GROUPS * 2 * (GH // 2) * SEQ])
        probs_t = place(C2, "probs_t", [P, 2, 2 * VT * P])
        o_ring = place(C2, "o_ring", [P, 2, 2, D])
        ot_ring = place(C2, "ot_ring", [P, 2, P])
        DD = C + 32768
        h_all = place(DD, "h_all", [P, TILES, D])
        D1 = DD + 1
        top[D1] = DD
        ctx_ring = place(D1, "ctx_ring", [P, 2, MT])
        xn_ring = place(D1, "xn_ring", [P, 2, 4, D])
        xnt_ring = place(D1, "xnt_ring", [P, 2, MT])
        D2 = DD + 2
        top[D2] = DD
        silu = place(D2, "silu", [P, 2, PS])
        gated = place(D2, "gated", [P, 2, PS])
        gated_hi = place(D2, "gated_hi", [P, 2, CHUNKS, PS], F32R)
        gated_lo = place(D2, "gated_lo", [P, 2, CHUNKS, PS], F32R)
        W = DD + 25600
        w13_raw = place(W, "w13_raw", [P, 2, 2, FFN])
        w2_raw = place(W, "w2_raw", [P, 2, CHUNKS, D])
        w13_hi = place(W, "w13_hi", [P, 2, 2, FFN], F32R)
        w13_lo = place(W, "w13_lo", [P, 2, 2, FFN], F32R)
        w2_hi = place(W, "w2_hi", [P, 2, CHUNKS, D], F32R)
        w2_lo = place(W, "w2_lo", [P, 2, CHUNKS, D], F32R)
        K = W + 33792
        const_sb = place(K, "const_sb", [P, sum(CONST_COLS.values())])
        wq_sb, wk_sb, wv_sb, wo_sb = (place(K, f"w{n}_sb", [P, D]) for n in "qkvo")
        gate_sb = place(K, "gate_sb", [P, EXPERTS])
        bq_sb, bk_sb, bv_sb = (place(K, f"b{n}_sb", [P, 1]) for n in "qkv")
        bo_sb = place(K, "bo_sb", [P, D])
        bv_rows = place(K, "bv_rows", [P, D])
        half_neg = place(K, "half_neg", [P, 4])
        stats = place(K, "stats", [P, 2, 4, 6])
        meanvar = place(K, "meanvar", [P, 2, 4, 2])
        var_eps = place(K, "var_eps", [P, 2, 4])
        rstd = place(K, "rstd", [P, 2, 4])
        row_max = place(K, "row_max", [P, 2, GROUPS * GH])
        rden = place(K, "rden", [P, 2, 2 * VT, 2])
        prob = place(K, "prob", [P, TILES, EXPERTS])
        places = place(K, "places", [P, TILES, EXPERTS])
        h_hi = place(K, "h_hi", [P, 2, 2 * D], F32R)
        h_lo = place(K, "h_lo", [P, 2, 2 * D], F32R)
        onehot = place(K, "onehot", [P, 2, 2, SLOTS], F32R)
        comb = place(K, "comb", [P, 2, 2, SLOTS])

        cv, at = {}, 0
        for name, cols in CONST_COLS.items():
            cv[name] = const_sb[:, at:at + cols]
            at += cols
        ident = cv["ident"]

        ps = stack.enter_context(nc.psum_tensor("ps", [P, 8, 512], F32))

        s_apart = sem("wait_carrier")
        N_CONST = 10
        s_const = sem("const_in")
        s_x = [sem(f"x_in{m}") for m in range(MACROS)]
        s_ctx = [sem(f"ctx_in{u}") for u in range(2)]
        s_w = [sem(f"weights_in{u}") for u in range(2)]
        s_vinit = sem("v_diag_zeroed")
        s_vones = sem("v_diag_ready")
        s_hneg = sem("half_neg_set")
        s_bvr = sem("bv_rows_ready")
        s_bop = sem("bo_product")
        s_bo = sem("bo_ready")
        s_bn = sem("stats_taken")
        s_mv = sem("meanvar_ready")
        s_ve = sem("var_eps_ready")
        s_rstd = sem("rstd_ready")
        s_xn = sem("xn_ready")
        s_xb = sem("residual_ready")
        s_xnt = sem("xnt_product")
        s_xntc = sem("xnt_ready")
        s_kp = sem("k_product")
        s_vp = sem("v_product")
        s_qp = sem("q_product")
        s_k = sem("k_ready")
        s_vl = sem("v_even_ready")
        s_vh = sem("v_odd_ready")
        s_q = sem("q_ready")
        s_qd = sem("q_diag_ready")
        s_kr = sem("k_ring_ready")
        s_sc = sem("scores_done")
        s_mx = sem("row_max_ready")
        s_sub = sem("shifted_ready")
        s_exp = sem("probs_ready")
        s_pt = sem("probs_turned")
        s_ptc = sem("probs_t_ready")
        s_av = sem("pv_done")
        s_rd = sem("rden_ready")
        s_o = sem("o_ready")
        s_ot = sem("o_turned")
        s_otc = sem("ot_ready")
        s_pj = sem("out_product")
        s_x1 = sem("x1_ready")
        s_bn2 = sem("stats2_taken")
        s_mv2 = sem("meanvar2_ready")
        s_ve2 = sem("var_eps2_ready")
        s_rstd2 = sem("rstd2_ready")
        s_h = sem("h_ready")
        s_hr = sem("h_ring_ready")
        s_htp = sem("ht_product")
        s_ht = sem("ht_ready")
        s_lgp = sem("logits_product")
        s_lg = sem("logits_ready")
        s_rt = sem("route_step")
        s_rexp = sem("route_exp")
        s_pos = sem("place_product")
        s_hhi = sem("h_hi_ready")
        s_hlo = sem("h_lo_ready")
        s_oh = sem("onehot_ready")
        s_cb = sem("comb_ready")
        s_g = [sem(f"gather_product{i}") for i in range(4)]
        s_gc = [sem(f"slots_ready{i}") for i in range(4)]
        s_ctp = sem("comb_turned")
        s_ctc = sem("comb_t_ready")
        s_whi = sem("weights_hi_ready")
        s_wlo = sem("weights_lo_ready")
        s_h1 = sem("up1_done")
        s_h3 = sem("up3_done")
        s_si = sem("silu_ready")
        s_gt = sem("gated_ready")
        s_ghi = sem("gated_hi_ready")
        s_glo = sem("gated_lo_ready")
        s_dn = sem("down_done")
        s_eo = sem("expert_out_ready")
        s_ci = [sem(f"combine_in{u}") for u in range(2)]
        s_cin = sem("combine_slots_in")
        s_st = sem("slots_turned")
        s_sr = sem("slot_rows_ready")
        s_cm = sem("combine_done")
        s_oc = sem("out_ready")
        s_os = [sem(f"out_stored{u}") for u in range(2)]

        def apart(eng):
            eng.sem_inc(s_apart, 1)

        def v_copies(copy, m, odd):
            for c in range(2):
                v_p = ps[odd * SEQ:(odd + 1) * SEQ, 3, :].rearrange("p (t n c) -> p t n c", t=4, n=VT)
                v_d = v_diag[c * SEQ:(c + 1) * SEQ, bass.ds(m * 8 * VT * VC, 8 * VT * VC)].rearrange(
                    "p (t b n c) -> p t b n c", t=4, b=2, n=VT)
                ins = copy(v_d[:, :, odd, :, 2 * HEAD * c:2 * HEAD * (c + 1)],
                           v_p[:, :, :, 2 * HEAD * c:2 * HEAD * (c + 1)])
            return ins

        block = stack.enter_context(nc.Block())

        @block.sync
        def _(sp):
            x_v = x.rearrange("(t p) d -> p t d", p=P)
            sp.dma_start(x_all[:, 0:4, :], x_v[:, 0:4, :]).then_inc(s_x[0], 16)
            sp.dma_start(const_sb[:, :], consts).then_inc(s_const, 16)

            def load_ctx(half, u):
                used(sp, s_vp, 2 * half + u - 1)
                sp.dma_start(ctx_ring[:, u, :], ctx_t[:, bass.ds((2 * half + u) * MT, MT)]).then_inc(s_ctx[u], 16)

            load_ctx(0, 0)
            for t, src in ((wk_sb, wk), (wv_sb, wv), (wq_sb, wq), (wo_sb, wo), (bq_sb, bq), (bk_sb, bk),
                           (bv_sb, bv), (bo_sb, bo)):
                sp.dma_start(t[:, :], src).then_inc(s_const, 16)
            sp.dma_start(gate_sb[:, :], gate).then_inc(s_const, 16)
            load_ctx(0, 1)
            for m in range(1, MACROS):
                sp.dma_start(x_all[:, 4 * m:4 * m + 4, :], x_v[:, 4 * m:4 * m + 4, :]).then_inc(s_x[m], 16)
            with sp.Fori(1, MACROS // 2) as half:
                load_ctx(half, 0)
                load_ctx(half, 1)

            def load_weights(half, u):
                used(sp, s_wlo, 2 * (2 * half + u - 1))
                e = 2 * half + u
                sp.dma_start(w13_raw[:, u, 0, :], w1[:, bass.ds(e * FFN, FFN)]).then_inc(s_w[u], 16)
                sp.dma_start(w13_raw[:, u, 1, :], w3[:, bass.ds(e * FFN, FFN)]).then_inc(s_w[u], 16)
                sp.dma_start(w2_raw[0:FC, u, :, :], w2[:, bass.ds(e * CHUNKS, CHUNKS), :]).then_inc(s_w[u], 16)

            load_weights(0, 0)
            load_weights(0, 1)
            with sp.Fori(1, EXPERTS // 2) as half:
                load_weights(half, 0)
                load_weights(half, 1)

            def load_combine(half, u):
                used(sp, s_cm, 2 * half + u - 1)
                m = 2 * half + u
                sp.dma_start(res_in[:, u, :, :], x1_all[:, bass.ds(4 * m, 4), :]).then_inc(s_ci[u], 16)

            sp.wait_ge(s_eo, EXPERTS * PARTS)
            load_combine(0, 0)
            load_combine(0, 1)

            def store(half, u):
                m = 2 * half + u
                sp.wait_ge(s_oc, m + 1)
                sp.dma_start(out_t[:, bass.ds(m * MT, MT)], out_ring[:, u, :]).then_inc(s_os[u], 16)

            with sp.Fori(1, MACROS // 2) as half:
                load_combine(half, 0)
                store(half - 1, 0)
                load_combine(half, 1)
                store(half - 1, 1)
            store(MACROS // 2 - 1, 0)
            store(MACROS // 2 - 1, 1)
            for u in range(2):
                sp.wait_ge(s_os[u], 16 * MACROS // 2)

        @block.gpsimd
        def _(pool):
            g = nc.gpsimd
            g.memset(half_neg[:, :], -0.5).then_inc(s_hneg, 1)
            pool.wait_ge(s_hneg, 1)

            def inverse_std(n, u, taken, ve, done):
                pool.wait_ge(taken, 4 * (n + 1))
                apart(pool)
                g.tensor_scalar(var_eps[:, u, :], meanvar[:, u, :, 1], EPS, None, ALU.add).then_inc(ve, 1)
                pool.wait_ge(ve, n + 1)
                g.tensor_tensor(rstd[:, u, :], var_eps[:, u, :], half_neg[:, :], ALU.pow).then_inc(done, 1)

            def ln1(half, u):
                n = 2 * half + u
                used(pool, s_xn, 4 * (n - 1))
                inverse_std(n, u, s_mv, s_ve, s_rstd)

            def v_clear():
                v_d = v_diag[:, :].rearrange("p (n c) -> p n c", c=VC)
                g.memset(v_diag[:, :], 0.0).then_inc(s_vinit, 1)
                pool.wait_ge(s_vinit, 1)
                g.memset(v_d[0:SEQ, :, VC - 2], 1.0).then_inc(s_vones, 1)
                pool.wait_ge(s_vones, 1)
                g.memset(v_d[SEQ:P, :, VC - 1], 1.0).then_inc(s_vones, 1)
                pool.wait_ge(s_vones, 2)

            def residual(half, u):
                m = 2 * half + u
                if isinstance(m, int) and m == 0:
                    pool.wait_ge(s_bo, 1)
                g.tensor_tensor(x1_all[:, bass.ds(4 * m, 4), :], x_all[:, bass.ds(4 * m, 4), :],
                                bo_sb[:, :].unsqueeze(1).to_broadcast([P, 4, D]), ALU.add).then_inc(s_xb, 1)

            ln1(0, 0)
            v_clear()
            ln1(0, 1)
            residual(0, 0)
            residual(0, 1)
            with pool.Fori(1, MACROS // 2) as half:
                ln1(half, 0)
                ln1(half, 1)
                residual(half, 0)
                residual(half, 1)

            def spread(half, u):
                s = 2 * half + u
                if isinstance(s, int) and s == 0:
                    pool.wait_ge(s_q, MACROS)
                    pool.wait_ge(s_k, MACROS)
                used(pool, s_sc, s - 1)
                g.tensor_tensor(q_diag[:, u, :, :, :],
                                q_all[:, bass.ds(s * P, P)].rearrange("p (b q) -> p b q", b=2).unsqueeze(2)
                                .to_broadcast([P, 2, GH, SEQ]),
                                cv["headmask"].unsqueeze(1).unsqueeze(3).to_broadcast([P, 2, GH, SEQ]),
                                ALU.mult).then_inc(s_qd, 1)
                apart(pool)
                g.tensor_copy(k_ring[:, u, :], k_all[:, bass.ds(s * P, P)]).then_inc(s_kr, 1)

            steps(pool, TILES, [(0, spread)])

            def ln2(half, u):
                n = 2 * half + u
                used(pool, s_h, 4 * (n - 1))
                inverse_std(n, u, s_mv2, s_ve2, s_rstd2)

            def h_copy(half, u):
                m = 2 * half + u
                pool.wait_ge(s_h, 4 * (m + 1))
                used(pool, s_htp, m - 1)
                apart(pool)
                g.tensor_copy(h_ring[:, u, :, :], h_all[:, bass.ds(4 * m, 4), :]).then_inc(s_hr, 1)

            steps(pool, MACROS, [(0, ln2), (1, h_copy)])

            def split_weights(half, u):
                e = 2 * half + u
                pool.wait_ge(s_w[u], 48 * (half + 1))
                used(pool, s_dn, PARTS * (e - 1))
                apart(pool)
                g.tensor_copy(w13_hi[:, u, :, :], w13_raw[:, u, :, :]).then_inc(s_whi, 1)
                g.tensor_copy(w2_hi[0:FC, u, :, :], w2_raw[0:FC, u, :, :]).then_inc(s_whi, 1)
                pool.wait_ge(s_whi, 2 * (e + 1))
                g.tensor_tensor(w13_lo[:, u, :, :], w13_raw[:, u, :, :], w13_hi[:, u, :, :],
                                ALU.subtract).then_inc(s_wlo, 1)
                g.tensor_tensor(w2_lo[0:FC, u, :, :], w2_raw[0:FC, u, :, :], w2_hi[0:FC, u, :, :],
                                ALU.subtract).then_inc(s_wlo, 1)

            split_weights(0, 0)
            split_weights(0, 1)

            def gather_parts(half, u):
                n = 2 * half + u
                used(pool, s_g[2], n - 1)
                used(pool, s_g[3], n - 1)
                apart(pool)
                g.tensor_copy(h_hi[:, u, :].rearrange("p (t d) -> p t d", t=2),
                              h_all[:, bass.ds(2 * n, 2), :]).then_inc(s_hhi, 1)
                pool.wait_ge(s_oh, n + 1)
                used(pool, s_ctp, n - 1)
                g.tensor_tensor(
                    comb[:, u, :, :].rearrange("p t (e c) -> p (t e) c", e=EXPERTS),
                    onehot[:, u, :, :].rearrange("p t (e c) -> p (t e) c", e=EXPERTS).bitcast(F32),
                    prob[:, bass.ds(2 * n, 2), :].rearrange("p t e -> p (t e)").unsqueeze(2)
                    .to_broadcast([P, 2 * EXPERTS, CAP]), ALU.mult).then_inc(s_cb, 1)

            steps(pool, UNITS, [(0, gather_parts)])
            with pool.Fori(1, EXPERTS // 2) as half:
                split_weights(half, 0)
                split_weights(half, 1)

            def combine_in(half, u):
                m = 2 * half + u
                if isinstance(m, int) and m == 0:
                    pool.wait_ge(s_eo, EXPERTS * PARTS)
                used(pool, s_st, 4 * (m - 1))
                apart(pool)
                g.tensor_copy(comb_in[:, u, :, :, :].rearrange("p b e c -> p e b c"),
                              expert_out[:, :].rearrange("p (e s) -> p e s", e=EXPERTS)[:, :, bass.ds(m * 8 * CAP, 8 * CAP)]
                              .rearrange("p e (b c) -> p e b c", b=8)).then_inc(s_cin, 1)

            steps(pool, MACROS, [(0, combine_in)])

        @block.scalar
        def _(act):
            s = nc.scalar
            act.wait_ge(s_const, 16 * N_CONST)

            def project_copies(half, u):
                m = 2 * half + u
                act.wait_ge(s_xnt, m + 1)
                used(act, s_qp, m - 1)
                s.copy(xnt_ring[:, u, :], ps[:, 0, :]).then_inc(s_xntc, 1)
                act.wait_ge(s_kp, m + 1)
                s.activation(k_all[:, bass.ds(m * MT, MT)], ps[:, 2, :], ACT.Identity,
                             bias=bk_sb[:, :]).then_inc(s_k, 1)
                act.wait_ge(s_vp, m + 1)
                if isinstance(m, int) and m == 0:
                    act.wait_ge(s_vones, 2)
                v_copies(s.copy, m, 0).then_inc(s_vl, 1)
                act.wait_ge(s_qp, m + 1)
                s.activation(q_all[:, bass.ds(m * MT, MT)], ps[:, 1, :], ACT.Identity,
                             bias=bq_sb[:, :]).then_inc(s_q, 1)

            steps(act, MACROS, [(0, project_copies)])

            def probs_copy(half, u):
                n = 2 * half + u
                act.wait_ge(s_pt, n + 1)
                used(act, s_av, n - 1)
                s.copy(probs_t[:, u, :].rearrange("p (b n) -> p b n", b=2), ps[:, 4:6, :]).then_inc(s_ptc, 1)

            def o_copy(half, u):
                n = 2 * half + u
                act.wait_ge(s_ot, n + 1)
                used(act, s_pj, n - 1)
                s.copy(ot_ring[:, u, :], ps[:, 6 + u, 320:320 + P]).then_inc(s_otc, 1)

            def exponential(half, u):
                n = 2 * half + u
                act.wait_ge(s_sub, n + 1)
                s.activation(probs[:, u, :], probs[:, u, :], ACT.Exp, scale=HEAD ** -0.5).then_inc(s_exp, 1)

            steps(act, TILES, [(1, probs_copy), (3, o_copy), (0, exponential)])

            def h_turn_copy(half, u):
                m = 2 * half + u
                act.wait_ge(s_htp, m + 1)
                used(act, s_lgp, m - 1)
                s.copy(ht_ring[:, u, :], ps[:, u, :]).then_inc(s_ht, 1)

            def logits_copy(half, u):
                m = 2 * half + u
                act.wait_ge(s_lgp, m + 1)
                s.copy(logits[:, bass.ds(4 * m, 4), :],
                       ps[:, 2 + u, 0:4 * EXPERTS].rearrange("p (t e) -> p t e", t=4)).then_inc(s_lg, 1)

            steps(act, MACROS, [(0, h_turn_copy), (1, logits_copy)])
            act.wait_ge(s_rt, 2)
            s.activation(rt[1][:, :, :], rt[0][:, :, :], ACT.Exp).then_inc(s_rexp, 1)

            hi_v = slots_hi[:, :].rearrange("p (e s) -> p e s", e=EXPERTS)

            def slots_copy(half, u):
                n = 2 * half + u
                for bank in range(2):
                    act.wait_ge(s_g[bank], n + 1)
                    for t in range(2):
                        src = ps[:, bank, t * SLOTS:(t + 1) * SLOTS].rearrange("p (e c) -> p e c", e=EXPERTS)
                        ins = s.copy(hi_v[:, :, bass.ds((4 * n + 2 * t + bank) * CAP, CAP)], src)
                    ins.then_inc(s_gc[bank], 1)
                act.wait_ge(s_ctp, n + 1)
                s.copy(comb_t[0:HALF, :, bass.ds(n * 2 * P, 2 * P)],
                       ps[0:HALF, 4 + u, :].rearrange("p (h n) -> p h n", h=2)).then_inc(s_ctc, 1)

            steps(act, UNITS, [(0, slots_copy)])

            def expert(half, u):
                for part in range(PARTS):
                    tile = (2 * half + u) * PARTS + part
                    for c in range(CHUNKS):
                        q = tile * CHUNKS + c
                        act.wait_ge(s_h1, q + 1)
                        used(act, s_gt, q - 1)
                        s.activation(silu[0:FC, c % 2, :], ps[0:FC, c % 2, 0:PS], ACT.Silu).then_inc(s_si, 1)
                        act.wait_ge(s_gt, q + 1)
                        if c == 0:
                            used(act, s_dn, tile - 1)
                        s.copy(gated_hi[0:FC, part % 2, c, :], gated[0:FC, c % 2, :]).then_inc(s_ghi, 1)

            expert(0, 0)
            expert(0, 1)
            with act.Fori(1, EXPERTS // 2) as half:
                expert(half, 0)
                expert(half, 1)

            def slot_copy(half, u):
                m = 2 * half + u
                for bank in range(0, 4, 2):
                    act.wait_ge(s_st, 4 * m + bank + 1)
                    used(act, s_cm, m)
                    s.copy(slot_rows[0:HALF, 4 * bank:4 * bank + 4, :],
                           ps[0:HALF, bank, :].rearrange("p (n d) -> p n d", n=4)).then_inc(s_sr, 1)

            steps(act, MACROS, [(0, slot_copy)])

        @block.vector
        def _(dve):
            v = nc.vector
            dve.wait_ge(s_const, 16 * N_CONST)
            v.tensor_scalar(bv_rows[:, :], cv["tri"], 0.0, bv_sb[:, 0:1], ALU.mult, ALU.add).then_inc(s_bvr, 1)

            def norm_stats(src, n, u, bn, mv):
                for t in range(4):
                    v.bn_stats(stats[:, u, t, :], src[:, bass.ds(4 * n + t, 1), :].rearrange("p t d -> p (t d)")
                               ).then_inc(bn, 1)
                dve.wait_ge(bn, 4 * (n + 1))
                apart(dve)
                for t in range(4):
                    v.bn_aggr(meanvar[:, u, t, :], stats[:, u, t, :]).then_inc(mv, 1)

            def ln1_stats(m):
                u = m % 2
                dve.wait_ge(s_x[m], 16)
                norm_stats(x_all, m, u, s_bn, s_mv)

            def ln1_apply(half, u):
                m = 2 * half + u
                dve.wait_ge(s_rstd, m + 1)
                used(dve, s_xnt, m - 1)
                for t in range(4):
                    v.tensor_scalar(xn_ring[:, u, t, :].unsqueeze(1), x_all[:, bass.ds(4 * m + t, 1), :],
                                    meanvar[:, u, t, 0:1], rstd[:, u, t:t + 1],
                                    ALU.subtract, ALU.mult).then_inc(s_xn, 1)

            def v_copy(half, u):
                m = 2 * half + u
                dve.wait_ge(s_vp, m + 1)
                if isinstance(m, int) and m == 0:
                    dve.wait_ge(s_vones, 2)
                v_copies(v.tensor_copy, m, 1).then_inc(s_vh, 1)

            for m in range(MACROS + 1):
                if m < MACROS:
                    used(dve, s_xn, 4 * (m - 1))
                    ln1_stats(m)
                if m == 1:
                    dve.wait_ge(s_bop, 1)
                    v.tensor_tensor(bo_sb[:, :], ps[:, 7, 0:D], bo_sb[:, :], ALU.add).then_inc(s_bo, 1)
                if m >= 1:
                    ln1_apply((m - 1) // 2, (m - 1) % 2)
                    v_copy((m - 1) // 2, (m - 1) % 2)

            NB = GROUPS * GH

            def shift(half, u):
                n = 2 * half + u
                sc = ps[:, 2 * u:2 * u + 2, :].rearrange("p g (n k) -> p (g n) k", k=SEQ)
                dve.wait_ge(s_sc, n + 1)
                v.tensor_reduce(row_max[:, u, :], sc, X, ALU.max).then_inc(s_mx, 1)
                dve.wait_ge(s_mx, n + 1)
                used(dve, s_pt, n - 1)
                v.tensor_tensor(probs[:, u, :].rearrange("p (n k) -> p n k", k=SEQ), sc,
                                row_max[:, u, :].unsqueeze(2).to_broadcast([P, NB, SEQ]),
                                ALU.subtract).then_inc(s_sub, 1)

            def add_residual(half, u):
                n = 2 * half + u
                if isinstance(n, int) and n == 0:
                    dve.wait_ge(s_xb, MACROS)
                dve.wait_ge(s_pj, n + 1)
                v.tensor_tensor(x1_all[:, bass.ds(n, 1), :], ps[:, 6 + u, 0:D].unsqueeze(1),
                                x1_all[:, bass.ds(n, 1), :], ALU.add).then_inc(s_x1, 1)

            def normalise(half, u):
                n = 2 * half + u
                pv = ps[:, 6 + u, 0:2 * VT * VC].rearrange("p (n c) -> p n c", c=VC)
                dve.wait_ge(s_av, n + 1)
                v.reciprocal(rden[:, u, :, :], pv[:, :, 4 * HEAD:VC]).then_inc(s_rd, 1)
                dve.wait_ge(s_rd, n + 1)
                used(dve, s_ot, n - 1)
                for h in range(2):
                    rows = slice(h * SEQ, (h + 1) * SEQ)
                    v.tensor_tensor(
                        o_ring[0:SEQ, u, :, :].rearrange("p b (t c h d) -> p (b t) c h d", c=2, h=2, d=HEAD)[:, :, :, h, :],
                        pv[rows, :, 0:4 * HEAD].rearrange("p n (c h d) -> p n c h d", c=2, h=2)[:, :, :, h, :],
                        rden[rows, u, :, :].unsqueeze(3).to_broadcast([SEQ, 2 * VT, 2, HEAD]),
                        ALU.mult).then_inc(s_o, 1)

            steps(dve, TILES, [(0, shift), (4, add_residual), (2, normalise)])

            def ln2_stats(half, u):
                n = 2 * half + u
                if isinstance(n, int) and n == 0:
                    dve.wait_ge(s_x1, TILES)
                used(dve, s_h, 4 * (n - 1))
                norm_stats(x1_all, n, u, s_bn2, s_mv2)

            def ln2_apply(half, u):
                m = 2 * half + u
                dve.wait_ge(s_rstd2, m + 1)
                for t in range(4):
                    v.tensor_scalar(h_all[:, bass.ds(4 * m + t, 1), :], x1_all[:, bass.ds(4 * m + t, 1), :],
                                    meanvar[:, u, t, 0:1], rstd[:, u, t:t + 1],
                                    ALU.subtract, ALU.mult).then_inc(s_h, 1)

            steps(dve, MACROS, [(0, ln2_stats), (1, ln2_apply)])

            done = [0]

            def then(ins):
                done[0] += 1
                ins.then_inc(s_rt, 1)
                dve.wait_ge(s_rt, done[0])

            def wide(a):
                return a[:, :].unsqueeze(2).to_broadcast([P, TILES, EXPERTS])

            rank = cv["rank"].unsqueeze(1).to_broadcast([P, TILES, EXPERTS])
            dve.wait_ge(s_lg, MACROS)
            then(v.tensor_reduce(rs[0][:, :], logits[:, :, :], X, ALU.max))
            then(v.tensor_tensor(rt[0][:, :, :], logits[:, :, :], wide(rs[0]), ALU.subtract))
            dve.wait_ge(s_rexp, 1)
            then(v.tensor_reduce(rs[1][:, :], rt[1][:, :, :], X, ALU.add))
            then(v.reciprocal(rs[2][:, :], rs[1][:, :]))
            then(v.tensor_tensor(prob[:, :, :], rt[1][:, :, :], wide(rs[2]), ALU.mult))

            def first_largest(values, largest, equal, weighted, best, chosen):
                then(v.tensor_reduce(largest[:, :], values[:, :, :], X, ALU.max))
                then(v.tensor_tensor(equal[:, :, :], values[:, :, :], wide(largest), ALU.is_equal))
                then(v.tensor_tensor(weighted[:, :, :], equal[:, :, :], rank, ALU.mult))
                then(v.tensor_reduce(best[:, :], weighted[:, :, :], X, ALU.max))
                then(v.tensor_tensor(chosen[:, :, :], weighted[:, :, :], wide(best), ALU.is_equal))

            first_largest(prob, rs[3], rt[2], rt[3], rs[4], rt[4])
            then(v.scalar_tensor_tensor(out=rt[5][:, :, :], in0=rt[4][:, :, :], scalar=-2.0, in1=prob[:, :, :],
                                        op0=ALU.mult, op1=ALU.add))
            first_largest(rt[5], rs[5], rt[2], rt[3], rs[0], rt[6])
            then(v.tensor_tensor(rt[7][:, :, :], rt[4][:, :, :], rt[6][:, :, :], ALU.add))
            dve.wait_ge(s_pos, 1)
            then(v.tensor_tensor(places[:, :, :], ps[:, 5, 0:TILES * EXPERTS].rearrange("p (t e) -> p t e", e=EXPERTS),
                                 rt[7][:, :, :], ALU.mult))

            lo_v = slots_lo[:, :].rearrange("p (e s) -> p e s", e=EXPERTS)

            def gather_parts(half, u):
                n = 2 * half + u
                used(dve, s_g[2], n - 1)
                used(dve, s_g[3], n - 1)
                used(dve, s_cb, n - 1)
                v.tensor_tensor(onehot[:, u, :, :].rearrange("p t (e c) -> p (t e) c", e=EXPERTS),
                                places[:, bass.ds(2 * n, 2), :].rearrange("p t e -> p (t e)").unsqueeze(2)
                                .to_broadcast([P, 2 * EXPERTS, CAP]),
                                cv["place"].unsqueeze(1).to_broadcast([P, 2 * EXPERTS, CAP]),
                                ALU.is_equal).then_inc(s_oh, 1)
                dve.wait_ge(s_hhi, n + 1)
                v.tensor_tensor(h_lo[:, u, :].rearrange("p (t d) -> p t d", t=2), h_all[:, bass.ds(2 * n, 2), :],
                                h_hi[:, u, :].rearrange("p (t d) -> p t d", t=2).bitcast(F32),
                                ALU.subtract).then_inc(s_hlo, 1)

            def slots_copy(half, u):
                n = 2 * half + u
                for bank in range(2):
                    dve.wait_ge(s_g[2 + bank], n + 1)
                    for t in range(2):
                        src = ps[:, 2 + bank, t * SLOTS:(t + 1) * SLOTS].rearrange("p (e c) -> p e c", e=EXPERTS)
                        ins = v.tensor_copy(lo_v[:, :, bass.ds((4 * n + 2 * t + bank) * CAP, CAP)], src)
                    ins.then_inc(s_gc[2 + bank], 1)

            steps(dve, UNITS, [(0, gather_parts), (1, slots_copy)])

            def expert_out_copy(tile, u):
                dve.wait_ge(s_dn, tile + 1)
                v.tensor_copy(expert_out[:, bass.ds(tile * PS, PS)], ps[:, 4 + u, 0:PS]).then_inc(s_eo, 1)

            def expert(half, u):
                for part in range(PARTS):
                    tile = (2 * half + u) * PARTS + part
                    for c in range(CHUNKS):
                        q = tile * CHUNKS + c
                        dve.wait_ge(s_h3, q + 1)
                        dve.wait_ge(s_si, q + 1)
                        used(dve, s_ghi, q - 1)
                        used(dve, s_glo, q - 1)
                        v.tensor_tensor(gated[0:FC, c % 2, :], ps[0:FC, 2 + c % 2, 0:PS], silu[0:FC, c % 2, :],
                                        ALU.mult).then_inc(s_gt, 1)
                        dve.wait_ge(s_ghi, q + 1)
                        if c == 0:
                            used(dve, s_dn, tile - 1)
                        v.tensor_tensor(gated_lo[0:FC, part % 2, c, :], gated[0:FC, c % 2, :],
                                        gated_hi[0:FC, part % 2, c, :].bitcast(F32),
                                        ALU.subtract).then_inc(s_glo, 1)
                        if c == 1:
                            if not isinstance(tile, int) or tile > 0:
                                expert_out_copy(tile - 1, (part - 1) % 2)

            dve.wait_ge(s_hlo, UNITS)
            dve.wait_ge(s_hhi, UNITS)
            expert(0, 0)
            expert(0, 1)
            with dve.Fori(1, EXPERTS // 2) as half:
                expert(half, 0)
                expert(half, 1)
            expert_out_copy(EXPERTS * PARTS - 1, 1)

            def slot_copy(half, u):
                m = 2 * half + u
                for bank in range(1, 4, 2):
                    dve.wait_ge(s_st, 4 * m + bank + 1)
                    used(dve, s_cm, m)
                    v.tensor_copy(slot_rows[0:HALF, 4 * bank:4 * bank + 4, :],
                                  ps[0:HALF, bank, :].rearrange("p (n d) -> p n d", n=4)).then_inc(s_sr, 1)

            def out_copy(half, u):
                m = 2 * half + u
                dve.wait_ge(s_cm, m + 1)
                used(dve, s_os[u], 16 * half)
                v.tensor_copy(out_ring[:, u, :], ps[:, 4 + u, :]).then_inc(s_oc, 1)

            steps(dve, MACROS, [(0, slot_copy), (1, out_copy)])

        @block.tensor
        def _(pe):
            mm = nc.tensor.matmul
            turn = nc.tensor.transpose
            pe.wait_ge(s_const, 16 * N_CONST)
            pe.wait_ge(s_bvr, 1)
            mm(ps[:, 7, 0:D], bv_rows[:, :], wo_sb[:, :], start=True, stop=True).then_inc(s_bop, 1)

            def project(half, u):
                m = 2 * half + u
                pe.wait_ge(s_xn, 4 * (m + 1))
                used(pe, s_xntc, m)
                for t in range(4):
                    ins = turn(ps[:, 0, t * P:(t + 1) * P], xn_ring[:, u, t, :], ident)
                ins.then_inc(s_xnt, 1)
                pe.wait_ge(s_ctx[u], 16 * (half + 1))
                used(pe, s_k, m)
                mm(ps[:, 2, :], wk_sb[:, :], ctx_ring[:, u, :], start=True, stop=True).then_inc(s_kp, 1)
                used(pe, s_vl, m)
                used(pe, s_vh, m)
                for t in range(4):
                    ins = mm(ps[:, 3, t * D:(t + 1) * D], ctx_ring[:, u, t * P:(t + 1) * P], wv_sb[:, :],
                             start=True, stop=True)
                ins.then_inc(s_vp, 1)
                pe.wait_ge(s_xntc, m + 1)
                used(pe, s_q, m)
                mm(ps[:, 1, :], wq_sb[:, :], xnt_ring[:, u, :], start=True, stop=True).then_inc(s_qp, 1)

            steps(pe, MACROS, [(0, project)])

            def scores(half, u):
                n = 2 * half + u
                if isinstance(n, int) and n == 0:
                    pe.wait_ge(s_q, MACROS)
                    pe.wait_ge(s_vl, MACROS)
                    pe.wait_ge(s_vh, MACROS)
                pe.wait_ge(s_qd, n + 1)
                pe.wait_ge(s_kr, n + 1)
                used(pe, s_sub, n - 1)
                for b in range(2):
                    for pair in range(GH // 2):
                        for g in range(GROUPS):
                            rows = slice(g * GH * HEAD, (g + 1) * GH * HEAD)
                            col = (b * (GH // 2) + pair) * SEQ
                            ins = mm(ps[:, 2 * u + g, col:col + SEQ],
                                     q_diag[rows, u, b, 2 * pair:2 * pair + 2, :].rearrange("p h q -> p (h q)"),
                                     k_ring[rows, u, b * SEQ:(b + 1) * SEQ], start=True, stop=True)
                ins.then_inc(s_sc, 1)

            def turn_probs(half, u):
                n = 2 * half + u
                pe.wait_ge(s_exp, n + 1)
                used(pe, s_ptc, n)
                for g in range(GROUPS):
                    for b in range(2):
                        for t2 in range(VT // GROUPS):
                            src = (g * GH + b * (GH // 2) + 2 * t2) * SEQ
                            to = (b * VT + g * (VT // GROUPS) + t2) * P
                            ins = turn(ps[:, 4 + to // 512, to % 512:to % 512 + P], probs[:, u, src:src + P], ident)
                ins.then_inc(s_pt, 1)

            def weigh(half, u):
                n = 2 * half + u
                pe.wait_ge(s_ptc, n + 1)
                used(pe, s_x1, n - 1)
                for i in range(2 * VT):
                    ins = mm(ps[:, 6 + u, i * VC:(i + 1) * VC], probs_t[:, u, i * P:(i + 1) * P],
                             v_diag[:, bass.ds((2 * VT * n + i) * VC, VC)], start=True, stop=True)
                ins.then_inc(s_av, 1)

            def turn_o(half, u):
                n = 2 * half + u
                pe.wait_ge(s_o, 2 * (n + 1))
                apart(pe)
                for b in range(2):
                    ins = turn(ps[:, 6 + u, 320 + b * SEQ:320 + (b + 1) * SEQ], o_ring[0:SEQ, u, b, :],
                               ident[0:SEQ, 0:SEQ])
                ins.then_inc(s_ot, 1)

            def out_product(half, u):
                n = 2 * half + u
                pe.wait_ge(s_otc, n + 1)
                mm(ps[:, 6 + u, 0:D], ot_ring[:, u, :], wo_sb[:, :], start=True, stop=True).then_inc(s_pj, 1)

            steps(pe, TILES, [(0, scores), (4, out_product), (1, turn_probs), (3, turn_o), (2, weigh)])

            def h_turn(half, u):
                m = 2 * half + u
                pe.wait_ge(s_hr, m + 1)
                used(pe, s_ht, m - 1)
                for t in range(4):
                    ins = turn(ps[:, u, t * P:(t + 1) * P], h_ring[:, u, t, :], ident)
                ins.then_inc(s_htp, 1)

            def route(half, u):
                m = 2 * half + u
                pe.wait_ge(s_ht, m + 1)
                used(pe, s_lg, m - 1)
                for t in range(4):
                    ins = mm(ps[:, 2 + u, t * EXPERTS:(t + 1) * EXPERTS], ht_ring[:, u, t * P:(t + 1) * P],
                             gate_sb[:, :], start=True, stop=True)
                ins.then_inc(s_lgp, 1)

            steps(pe, MACROS, [(0, h_turn), (1, route)])

            pe.wait_ge(s_rt, 17)
            mm(ps[:, 5, 0:TILES * EXPERTS], cv["tri"], rt[7][:, :, :], start=True, stop=True).then_inc(s_pos, 1)

            def gather(half, u):
                n = 2 * half + u
                if isinstance(n, int) and n == 0:
                    pe.wait_ge(s_lg, MACROS)
                pe.wait_ge(s_oh, n + 1)
                pe.wait_ge(s_hhi, n + 1)
                for lo in range(2):
                    if lo:
                        pe.wait_ge(s_hlo, n + 1)
                    part = h_lo if lo else h_hi
                    for odd in range(2):
                        used(pe, s_gc[2 * lo + odd], n)
                    for t in range(2):
                        for odd in range(2):
                            rows = slice(odd * SEQ, (odd + 1) * SEQ)
                            ins = mm(ps[:, 2 * lo + odd, t * SLOTS:(t + 1) * SLOTS], part[rows, u, t * D:(t + 1) * D],
                                     onehot[rows, u, t, :], start=True, stop=True)
                            if t:
                                ins.then_inc(s_g[2 * lo + odd], 1)

            def turn_comb(half, u):
                n = 2 * half + u
                pe.wait_ge(s_cb, n + 1)
                used(pe, s_ctc, n - 1)
                if isinstance(n, int) and n == 1:
                    pe.wait_ge(s_rt, 18)
                for h in range(2):
                    for t in range(2):
                        ins = turn(ps[0:HALF, 4 + u, (2 * h + t) * P:(2 * h + t + 1) * P],
                                   comb[:, u, t, h * HALF:(h + 1) * HALF], ident)
                ins.then_inc(s_ctp, 1)

            steps(pe, UNITS, [(0, gather), (1, turn_comb)])

            def up(tile, e_off, part, u):
                for c in range(CHUNKS):
                    q = tile * CHUNKS + c
                    for w, free, done in ((0, s_si, s_h1), (1, s_gt, s_h3)):
                        used(pe, free, q - 1)
                        bank = ps[0:FC, 2 * w + c % 2, 0:PS]
                        cols = slice(c * FC, (c + 1) * FC)
                        hi = slots_hi[:, bass.ds(tile * PS, PS)]
                        lo = slots_lo[:, bass.ds(tile * PS, PS)]
                        mm(bank, w13_lo[:, u, w, cols], hi, start=True, stop=False)
                        mm(bank, w13_hi[:, u, w, cols], lo, start=False, stop=False)
                        mm(bank, w13_hi[:, u, w, cols], hi, start=False, stop=True).then_inc(done, 1)

            def down(tile, part, u):
                used(pe, s_eo, tile - 1)
                bank = ps[:, 4 + part % 2, 0:PS]
                for c in range(CHUNKS):
                    pe.wait_ge(s_ghi, tile * CHUNKS + c + 1)
                    mm(bank, w2_lo[0:FC, u, c, :], gated_hi[0:FC, part % 2, c, :], start=(c == 0), stop=False)
                    mm(bank, w2_hi[0:FC, u, c, :], gated_hi[0:FC, part % 2, c, :], start=False, stop=False)
                    pe.wait_ge(s_glo, tile * CHUNKS + c + 1)
                    ins = mm(bank, w2_hi[0:FC, u, c, :], gated_lo[0:FC, part % 2, c, :], start=False,
                             stop=(c == CHUNKS - 1))
                ins.then_inc(s_dn, 1)

            def expert(half, u):
                e = 2 * half + u
                for part in range(PARTS):
                    tile = e * PARTS + part
                    if part == 0:
                        pe.wait_ge(s_wlo, 2 * (e + 1))
                    up(tile, 0, part, u)
                    if not isinstance(tile, int) or tile > 0:
                        down(tile - 1, (part - 1) % PARTS, u if part else 1 - u)

            pe.wait_ge(s_ctc, UNITS)
            for i in range(4):
                pe.wait_ge(s_gc[i], UNITS)
            expert(0, 0)
            expert(0, 1)
            with pe.Fori(1, EXPERTS // 2) as half:
                expert(half, 0)
                expert(half, 1)
            down(EXPERTS * PARTS - 1, PARTS - 1, 1)

            def turn_slots(half, u):
                m = 2 * half + u
                pe.wait_ge(s_cin, m + 1)
                for bank in range(4):
                    used(pe, s_sr, 4 * m)
                    for i in range(4):
                        b, h = (4 * bank + i) // 2, i % 2
                        ins = turn(ps[0:HALF, bank, i * D:(i + 1) * D],
                                   comb_in[:, u, b, 4 * h:4 * h + 4, :].rearrange("p e c -> p (e c)"), ident)
                    ins.then_inc(s_st, 1)

            def combine(half, u):
                m = 2 * half + u
                pe.wait_ge(s_sr, 4 * (m + 1))
                pe.wait_ge(s_ci[u], 16 * (half + 1))
                used(pe, s_oc, m - 1)
                for t in range(4):
                    mm(ps[:, 4 + u, t * P:(t + 1) * P], res_in[:, u, t, :], ident, start=(t == 0), stop=False,
                       skip_group_check=True)
                for b in range(8):
                    for h in range(2):
                        ins = mm(ps[:, 4 + u, b * SEQ:(b + 1) * SEQ], slot_rows[0:HALF, 2 * b + h, :],
                                 comb_t[0:HALF, h, bass.ds(m * MT + b * SEQ, SEQ)],
                                 start=False, stop=(b == 7 and h == 1), skip_group_check=True)
                ins.then_inc(s_cm, 1)

            steps(pe, MACROS, [(0, turn_slots), (0, combine)])


def kernel(**inputs):
    import numpy as _np
    import concourse.bacc as _bacc
    from concourse import mybir as _mybir
    from concourse.bass_utils import run_bass_kernel_spmd as _run

    def laid(name):
        return _np.asarray(inputs[name])

    def weight(name):
        return _np.ascontiguousarray(laid(name).T)

    def column(name):
        return _np.ascontiguousarray(laid(name).reshape(-1, 1))

    arrays = {
        "x": laid("x").reshape(TOKENS, D),
        "ctx_t": _np.ascontiguousarray(laid("ctx_1024").reshape(TOKENS, D).T),
        "consts": constants(),
        "wq": weight("L0_xattn_Wq"),
        "wk": weight("L0_xattn_Wk"),
        "wv": weight("L0_xattn_Wv"),
        "wo": weight("L0_xattn_Wo"),
        "bq": column("L0_xattn_bq"),
        "bk": column("L0_xattn_bk"),
        "bv": column("L0_xattn_bv"),
        "bo": _np.ascontiguousarray(_np.broadcast_to(laid("L0_xattn_bo"), (P, D))),
        "gate": weight("L0_ffn_gate_w"),
        "w1": _np.ascontiguousarray(laid("L0_ffn_w1").transpose(1, 0, 2).reshape(D, EXPERTS * FFN)),
        "w2": _np.ascontiguousarray(
            laid("L0_ffn_w2").reshape(EXPERTS * CHUNKS, FC, D).transpose(1, 0, 2)),
        "w3": _np.ascontiguousarray(laid("L0_ffn_w3").transpose(1, 0, 2).reshape(D, EXPERTS * FFN)),
    }
    nc = _bacc.Bacc("TRN2", target_bir_lowering=False, num_devices=1)
    args = [nc.dram_tensor(f"in_{n}", a.shape, _mybir.dt.from_np(a.dtype), kind="ExternalInput").ap()
            for n, a in arrays.items()]
    out = nc.dram_tensor("out_t", (D, TOKENS), _mybir.dt.float32, kind="ExternalOutput").ap()
    build(nc, *args, out)
    r = _run(nc, [{f"in_{n}": a for n, a in arrays.items()}], core_ids=[0])
    return _np.ascontiguousarray(r.results[0]["out_t"].T).reshape(SEQS, SEQ, D)
```

```python
from contextlib import ExitStack

import numpy as np

import concourse.bass as bass
from concourse import mybir

ALU = mybir.AluOpType
ACT = mybir.ActivationFunctionType
F32 = mybir.dt.float32
F32R = mybir.dt.float32r
X = mybir.AxisListType.X

SEQS, SEQ, D = 64, 64, 128
HEADS = 16
HEAD = D // HEADS
EXPERTS, TOPK, FFN = 8, 2, 448
CAP = int(SEQ * TOPK / EXPERTS * 1.25)
EPS = 1e-5

P = 128
TOKENS = SEQS * SEQ
TILES = TOKENS // P
MACROS = TILES // 4
UNITS = TILES // 2
MT = 4 * P
GROUPS = 2
GH = HEADS // GROUPS
PAIRS = GH // 2
SLOTS = EXPERTS * CAP
HALF = SLOTS // 2
ESLOTS = SEQS * CAP
PARTS = 4
PS = ESLOTS // PARTS
CHUNKS = 4
FC = FFN // CHUNKS
CONST_COLS = dict(ident=P, tri=P, headmask=GH, place=CAP, rank=EXPERTS)


def constants():
    p = np.arange(P)
    parts = dict(
        ident=np.eye(P),
        tri=(p[:, None] // SEQ == p[None, :] // SEQ) & (p[:, None] <= p[None, :]),
        headmask=(p[:, None] % (GH * HEAD)) // HEAD == np.arange(GH)[None, :],
        place=np.tile(np.arange(1, CAP + 1), (P, 1)),
        rank=np.tile(np.arange(EXPERTS, 0, -1), (P, 1)),
    )
    return np.concatenate([np.asarray(parts[n], np.float32) for n in CONST_COLS], axis=1)


def used(eng, semaphore, count):
    if not isinstance(count, int) or count > 0:
        eng.wait_ge(semaphore, count)


def steps(eng, n, stages):
    depth = max(lag for lag, _ in stages)
    head = (depth + 3) // 2

    def slot(pair, u):
        for lag, stage in stages:
            parity = (u - lag) % 2
            half = pair + (u - lag - parity) // 2
            if isinstance(pair, int) and not 0 <= 2 * half + parity < n:
                continue
            stage(half, parity)

    for pair in range(min(head, n // 2)):
        slot(pair, 0)
        slot(pair, 1)
    if head < n // 2:
        with eng.Fori(head, n // 2) as pair:
            slot(pair, 0)
            slot(pair, 1)
    for t in range(n, n + depth):
        slot(t // 2, t % 2)


def build(nc, x, ctx_t, consts, wq, wk, wv, wo, bq, bk, bv, bo, gate, w1, w2, w3, out):
    with ExitStack() as stack:
        sem_names = {}

        def sem(name):
            sem_names[name] = stack.enter_context(nc.semaphore(name))
            return sem_names[name]

        ARENA = 212000
        arena = -(-nc.sbuf_base // 64) * 64
        stack.enter_context(nc.sbuf_tensor("arena", [P, ARENA], mybir.dt.uint8, align_bytes=64))
        top = {}

        def place(region, name, shape, dtype=F32):
            at = top.get(region, region)
            size = 4 * int(np.prod(shape[1:]))
            top[region] = at + size
            assert at + size <= ARENA, name
            at += -at % 32
            top[region] = at + size
            return nc.alloc_sbuf_tensor_at(name, shape, dtype, offset=arena + at)

        A = 0
        q_all = place(A, "q_all", [P, TOKENS])
        k_all = place(A, "k_all", [P, TOKENS])
        v_all = place(A, "v_all", [P, TILES, D])
        x_all = place(A, "x_all", [P, TILES, D])
        A2 = 1
        top[A2] = 0
        slots_hi = place(A2, "slots_hi", [P, SEQS * SLOTS], F32R)
        slots_lo = place(A2, "slots_lo", [P, SEQS * SLOTS], F32R)
        A3 = 2
        top[A3] = 0
        expert_out = place(A3, "expert_out", [P, SEQS * SLOTS])
        slot_rows = place(A3, "slot_rows", [P, 2, 16, D])
        out_ring = place(A3, "out_ring", [P, 2, 4, D])
        A4 = 3
        top[A4] = 0
        h_all = place(A4, "h_all", [P, TILES, D])
        ht_ring = place(A4, "ht_ring", [P, 2, MT])
        logits = place(A4, "logits", [P, TILES, EXPERTS])
        rt = [place(A4, f"route_{i}", [P, TILES, EXPERTS]) for i in range(8)]
        rs = [place(A4, f"route_s{i}", [P, TILES]) for i in range(6)]

        B = 81920
        x1_all = place(B, "x1_all", [P, TILES, D])
        C = B + 16384
        comb_t = place(C, "comb_t", [P, 2, TOKENS])
        C2 = C + 1
        top[C2] = C
        q_diag = place(C2, "q_diag", [P, 2, 2, P])
        k_diag = place(C2, "k_diag", [P, 2, 2, GH, SEQ])
        probs = place(C2, "probs", [P, 2, 2 * GH * SEQ])
        probs_t = place(C2, "probs_t", [P, 2, 2 * PAIRS * P])
        v_diag = place(C2, "v_diag", [P, 2, 2, GROUPS, PAIRS, 32])
        ot_ring = place(C2, "ot_ring", [P, 2, P])
        DD = C + 32768
        h_hi = place(DD, "h_hi", [P, TILES, D], F32R)
        h_lo = place(DD, "h_lo", [P, TILES, D], F32R)
        D1 = DD + 1
        top[D1] = DD
        ctx_ring = place(D1, "ctx_ring", [P, 2, MT])
        xn_ring = place(D1, "xn_ring", [P, 2, 4, D])
        xnt_ring = place(D1, "xnt_ring", [P, 2, MT])
        D2 = DD + 2
        top[D2] = DD
        silu = place(D2, "silu", [P, 2, PS])
        gated = place(D2, "gated", [P, 2, PS])
        gated_hi = place(D2, "gated_hi", [P, 2, CHUNKS, PS], F32R)
        gated_lo = place(D2, "gated_lo", [P, 2, CHUNKS, PS], F32R)
        W = DD + 32768
        w13_raw = place(W, "w13_raw", [P, 2, 2, FFN])
        w2_raw = place(W, "w2_raw", [P, 2, CHUNKS, D])
        w13_hi = place(W, "w13_hi", [P, 2, 2, FFN], F32R)
        w13_lo = place(W, "w13_lo", [P, 2, 2, FFN], F32R)
        w2_hi = place(W, "w2_hi", [P, 2, CHUNKS, D], F32R)
        w2_lo = place(W, "w2_lo", [P, 2, CHUNKS, D], F32R)
        K = W + 33792
        const_sb = place(K, "const_sb", [P, sum(CONST_COLS.values())])
        wq_sb, wk_sb, wv_sb, wo_sb = (place(K, f"w{n}_sb", [P, D]) for n in "qkvo")
        gate_sb = place(K, "gate_sb", [P, EXPERTS])
        bq_sb, bk_sb, bv_sb = (place(K, f"b{n}_sb", [P, 1]) for n in "qkv")
        bo_sb = place(K, "bo_sb", [P, D])
        bv_rows = place(K, "bv_rows", [P, D])
        half_neg = place(K, "half_neg", [P, 4])
        stats = place(K, "stats", [P, 2, 4, 6])
        meanvar = place(K, "meanvar", [P, 2, 4, 2])
        var_eps = place(K, "var_eps", [P, 2, 4])
        rstd = place(K, "rstd", [P, 2, 4])
        row_max = place(K, "row_max", [P, 2, 2 * GH])
        row_sum = place(K, "row_sum", [P, 2, 2 * GH])
        rden = place(K, "rden", [P, 2, 2 * GH])
        prob = place(K, "prob", [P, TILES, EXPERTS])
        places = place(K, "places", [P, TILES, EXPERTS])
        onehot = place(K, "onehot", [P, 2, 2, SLOTS], F32R)
        comb = place(K, "comb", [P, 2, 2, SLOTS])

        cv, at = {}, 0
        for name, cols in CONST_COLS.items():
            cv[name] = const_sb[:, at:at + cols]
            at += cols
        ident = cv["ident"]

        ps = stack.enter_context(nc.psum_tensor("ps", [P, 8, 512], F32))

        s_apart = sem("wait_carrier")
        N_CONST = 10
        s_const = sem("const_in")
        s_x = [sem(f"x_in{m}") for m in range(MACROS)]
        s_ctx = [sem(f"ctx_in{u}") for u in range(2)]
        s_w = [sem(f"weights_in{u}") for u in range(2)]
        s_zero = sem("diagonals_cleared")
        s_hneg = sem("half_neg_set")
        s_bvr = sem("bv_rows_ready")
        s_bop = sem("bo_product")
        s_bo = sem("bo_ready")
        s_bn = sem("stats_taken")
        s_mv = sem("meanvar_ready")
        s_ve = sem("var_eps_ready")
        s_rstd = sem("rstd_ready")
        s_xn = sem("xn_ready")
        s_xb = sem("residual_ready")
        s_xnt = sem("xnt_product")
        s_xntc = sem("xnt_ready")
        s_kp = sem("k_product")
        s_vp = sem("v_product")
        s_qp = sem("q_product")
        s_k = sem("k_ready")
        s_v = sem("v_ready")
        s_q = sem("q_ready")
        s_kd = sem("k_diag_ready")
        s_qd = sem("q_diag_ready")
        s_vd = sem("v_diag_ready")
        s_sc = sem("scores_done")
        s_mx = sem("row_max_ready")
        s_sub = sem("shifted_ready")
        s_exp = sem("exp_ready")
        s_sum = sem("row_sum_ready")
        s_rd = sem("rden_ready")
        s_pn = sem("probs_ready")
        s_pt = sem("probs_turned")
        s_ptc = sem("probs_t_ready")
        s_av = sem("pv_done")
        s_otc = sem("ot_ready")
        s_pj = sem("out_product")
        s_x1 = sem("x1_ready")
        s_bn2 = sem("stats2_taken")
        s_mv2 = sem("meanvar2_ready")
        s_ve2 = sem("var_eps2_ready")
        s_rstd2 = sem("rstd2_ready")
        s_h = sem("h_ready")
        s_htp = sem("ht_product")
        s_ht = sem("ht_ready")
        s_lgp = sem("logits_product")
        s_lg = sem("logits_ready")
        s_rt = sem("route_step")
        s_rexp = sem("route_exp")
        s_pos = sem("place_product")
        s_hhi = sem("h_hi_ready")
        s_hlo = sem("h_lo_ready")
        s_oh = sem("onehot_ready")
        s_cb = sem("comb_ready")
        s_g = [sem(f"gather_product{i}") for i in range(4)]
        s_gc = [sem(f"slots_ready{i}") for i in range(4)]
        s_ctp = sem("comb_turned")
        s_ctc = sem("comb_t_ready")
        s_whi = sem("weights_hi_ready")
        s_wlo = sem("weights_lo_ready")
        s_h1 = sem("up1_done")
        s_h3 = sem("up3_done")
        s_si = sem("silu_ready")
        s_gt = sem("gated_ready")
        s_ghi = sem("gated_hi_ready")
        s_glo = sem("gated_lo_ready")
        s_dn = sem("down_done")
        s_eo = sem("expert_out_ready")
        s_st = [sem(f"slots_turned{i}") for i in range(4)]
        s_sr = [sem(f"slot_rows_ready{i}") for i in range(4)]
        s_cm = sem("combine_done")
        s_oc = sem("out_ready")
        s_os = [sem(f"out_stored{u}") for u in range(2)]

        def apart(eng):
            eng.sem_inc(s_apart, 1)

        def slots_at(slots, n, odd):
            return slots[:, bass.ds(n * 4 * SLOTS, 4 * SLOTS)].rearrange("p (t s) -> p t s", t=2)[
                :, :, odd * SLOTS:(odd + 1) * SLOTS]

        def expert_slots(slots, e, part):
            seqs = SEQS // PARTS
            return slots[:, :].rearrange("p (b s) -> p b s", b=SEQS)[
                :, part * seqs:(part + 1) * seqs, bass.ds(e * CAP, CAP)]

        BANKS = 3
        PER_LOOP = 2 * PARTS * CHUNKS

        def before(at):
            return BANKS if at >= BANKS else next(
                at + PER_LOOP - i for i in range(PER_LOOP - 1, -1, -1) if i % BANKS == at)

        block = stack.enter_context(nc.Block())

        @block.sync
        def _(sp):
            x_v = x.rearrange("(t p) d -> p t d", p=P)
            sp.dma_start(x_all[:, 0:4, :], x_v[:, 0:4, :]).then_inc(s_x[0], 16)
            sp.dma_start(const_sb[:, :], consts).then_inc(s_const, 16)

            def load_ctx(half, u):
                used(sp, s_vp, 2 * half + u - 1)
                sp.dma_start(ctx_ring[:, u, :], ctx_t[:, bass.ds((2 * half + u) * MT, MT)]).then_inc(s_ctx[u], 16)

            load_ctx(0, 0)
            for t, src in ((wk_sb, wk), (wv_sb, wv), (wq_sb, wq), (wo_sb, wo), (bq_sb, bq), (bk_sb, bk),
                           (bv_sb, bv), (bo_sb, bo)):
                sp.dma_start(t[:, :], src).then_inc(s_const, 16)
            sp.dma_start(gate_sb[:, :], gate).then_inc(s_const, 16)
            load_ctx(0, 1)
            for m in range(1, MACROS):
                sp.dma_start(x_all[:, 4 * m:4 * m + 4, :], x_v[:, 4 * m:4 * m + 4, :]).then_inc(s_x[m], 16)
            with sp.Fori(1, MACROS // 2) as half:
                load_ctx(half, 0)
                load_ctx(half, 1)

            def load_weights(half, u):
                used(sp, s_wlo, 2 * (2 * half + u - 1))
                e = 2 * half + u
                sp.dma_start(w13_raw[:, u, 0, :], w1[:, bass.ds(e * FFN, FFN)]).then_inc(s_w[u], 16)
                sp.dma_start(w13_raw[:, u, 1, :], w3[:, bass.ds(e * FFN, FFN)]).then_inc(s_w[u], 16)
                sp.dma_start(w2_raw[0:FC, u, :, :], w2[:, bass.ds(e * CHUNKS, CHUNKS), :]).then_inc(s_w[u], 16)

            load_weights(0, 0)
            load_weights(0, 1)
            with sp.Fori(1, EXPERTS // 2) as half:
                load_weights(half, 0)
                load_weights(half, 1)

            out_v = out.rearrange("(t p) d -> p t d", p=P)

            def store(half, u):
                m = 2 * half + u
                sp.wait_ge(s_oc, m + 1)
                sp.dma_start(out_v[:, bass.ds(4 * m, 4), :], out_ring[:, u, :, :]).then_inc(s_os[u], 16)

            store(0, 0)
            store(0, 1)
            with sp.Fori(1, MACROS // 2) as half:
                store(half, 0)
                store(half, 1)
            for u in range(2):
                sp.wait_ge(s_os[u], 16 * MACROS // 2)

        @block.gpsimd
        def _(pool):
            g = nc.gpsimd
            g.memset(half_neg[:, :], -0.5).then_inc(s_hneg, 1)
            pool.wait_ge(s_hneg, 1)

            def inverse_std(n, u, taken, ve, done):
                pool.wait_ge(taken, 4 * (n + 1))
                apart(pool)
                g.tensor_scalar(var_eps[:, u, :], meanvar[:, u, :, 1], EPS, None, ALU.add).then_inc(ve, 1)
                pool.wait_ge(ve, n + 1)
                g.tensor_tensor(rstd[:, u, :], var_eps[:, u, :], half_neg[:, :], ALU.pow).then_inc(done, 1)

            def ln1(half, u):
                n = 2 * half + u
                used(pool, s_xn, 4 * (n - 1))
                inverse_std(n, u, s_mv, s_ve, s_rstd)

            def clear_diagonals():
                g.memset(q_diag[:, :, :, :], 0.0).then_inc(s_zero, 1)
                g.memset(v_diag[:, :, :, :, :, :], 0.0).then_inc(s_zero, 1)

            def residual(half, u):
                m = 2 * half + u
                if isinstance(m, int) and m == 0:
                    pool.wait_ge(s_bo, 1)
                g.tensor_tensor(x1_all[:, bass.ds(4 * m, 4), :], x_all[:, bass.ds(4 * m, 4), :],
                                bo_sb[:, :].unsqueeze(1).to_broadcast([P, 4, D]), ALU.add).then_inc(s_xb, 1)

            ln1(0, 0)
            clear_diagonals()
            ln1(0, 1)
            residual(0, 0)
            residual(0, 1)
            with pool.Fori(1, MACROS // 2) as half:
                ln1(half, 0)
                ln1(half, 1)
                residual(half, 0)
                residual(half, 1)

            def spread_k(half, u):
                s = 2 * half + u
                if isinstance(s, int) and s == 0:
                    pool.wait_ge(s_k, MACROS)
                used(pool, s_sc, s - 1)
                g.tensor_tensor(k_diag[:, u, :, :, :],
                                k_all[:, bass.ds(s * P, P)].rearrange("p (b k) -> p b k", b=2).unsqueeze(2)
                                .to_broadcast([P, 2, GH, SEQ]),
                                cv["headmask"].unsqueeze(1).unsqueeze(3).to_broadcast([P, 2, GH, SEQ]),
                                ALU.mult).then_inc(s_kd, 1)

            def normalise(half, u):
                n = 2 * half + u
                pool.wait_ge(s_rd, n + 1)
                e = probs[:, u, :].rearrange("p (n k) -> p n k", k=SEQ)
                g.tensor_tensor(e, e, rden[:, u, :].unsqueeze(2).to_broadcast([P, 2 * GH, SEQ]),
                                ALU.mult).then_inc(s_pn, 1)

            steps(pool, TILES, [(0, spread_k), (2, normalise)])

            def ln2(half, u):
                n = 2 * half + u
                used(pool, s_h, 4 * (n - 1))
                inverse_std(n, u, s_mv2, s_ve2, s_rstd2)

            steps(pool, MACROS, [(0, ln2)])

            def split_weights(half, u):
                e = 2 * half + u
                pool.wait_ge(s_w[u], 48 * (half + 1))
                used(pool, s_dn, PARTS * (e - 1))
                apart(pool)
                g.tensor_copy(w13_hi[:, u, :, :], w13_raw[:, u, :, :]).then_inc(s_whi, 1)
                g.tensor_copy(w2_hi[0:FC, u, :, :], w2_raw[0:FC, u, :, :]).then_inc(s_whi, 1)
                pool.wait_ge(s_whi, 2 * (e + 1))
                g.tensor_tensor(w13_lo[:, u, :, :], w13_raw[:, u, :, :], w13_hi[:, u, :, :],
                                ALU.subtract).then_inc(s_wlo, 1)
                g.tensor_tensor(w2_lo[0:FC, u, :, :], w2_raw[0:FC, u, :, :], w2_hi[0:FC, u, :, :],
                                ALU.subtract).then_inc(s_wlo, 1)

            split_weights(0, 0)
            split_weights(0, 1)

            def weigh_onehot(half, u):
                n = 2 * half + u
                pool.wait_ge(s_oh, n + 1)
                used(pool, s_ctp, n - 1)
                g.tensor_tensor(
                    comb[:, u, :, :].rearrange("p t (e c) -> p (t e) c", e=EXPERTS),
                    onehot[:, u, :, :].rearrange("p t (e c) -> p (t e) c", e=EXPERTS).bitcast(F32),
                    prob[:, bass.ds(2 * n, 2), :].rearrange("p t e -> p (t e)").unsqueeze(2)
                    .to_broadcast([P, 2 * EXPERTS, CAP]), ALU.mult).then_inc(s_cb, 1)

            steps(pool, UNITS, [(0, weigh_onehot)])
            with pool.Fori(1, EXPERTS // 2) as half:
                split_weights(half, 0)
                split_weights(half, 1)

        @block.scalar
        def _(act):
            s = nc.scalar
            act.wait_ge(s_const, 16 * N_CONST)

            def project_copies(half, u):
                m = 2 * half + u
                act.wait_ge(s_kp, m + 1)
                s.activation(k_all[:, bass.ds(m * MT, MT)], ps[:, 2, :], ACT.Identity,
                             bias=bk_sb[:, :]).then_inc(s_k, 1)
                act.wait_ge(s_xnt, m + 1)
                used(act, s_qp, m - 1)
                s.copy(xnt_ring[:, u, :], ps[:, 0, :]).then_inc(s_xntc, 1)
                act.wait_ge(s_vp, m + 1)
                s.copy(v_all[:, bass.ds(4 * m, 4), :], ps[:, 3, :].rearrange("p (t d) -> p t d", t=4)
                       ).then_inc(s_v, 1)

            def q_copy(half, u):
                m = 2 * half + u
                act.wait_ge(s_qp, m + 1)
                s.activation(q_all[:, bass.ds(m * MT, MT)], ps[:, 1, :], ACT.Identity,
                             bias=bq_sb[:, :]).then_inc(s_q, 1)

            steps(act, MACROS, [(0, project_copies), (1, q_copy)])

            def spread_q(half, u):
                n = 2 * half + u
                if isinstance(n, int) and n == 0:
                    act.wait_ge(s_zero, 2)
                    act.wait_ge(s_q, MACROS)
                    act.wait_ge(s_v, MACROS)
                used(act, s_sc, n - 1)
                for g in range(GROUPS):
                    rows = slice(g * SEQ, (g + 1) * SEQ)
                    ins = s.copy(q_diag[rows, u, :, g * SEQ:(g + 1) * SEQ],
                                 q_all[rows, bass.ds(n * P, P)].rearrange("p (b q) -> p b q", b=2))
                ins.then_inc(s_qd, 1)

            def spread_v(half, u):
                n = 2 * half + u
                used(act, s_av, n - 1)
                for b in range(2):
                    src = v_all[b * SEQ:(b + 1) * SEQ, bass.ds(n, 1), :].rearrange(
                        "p o (g c h d) -> p (o g) c h d", g=2 * GROUPS, c=2, h=2)
                    for h in range(2):
                        to = v_diag[h * SEQ:(h + 1) * SEQ, u, b, :, :, :].rearrange("p g c n -> p (g c n)")
                        to = to.rearrange("p (g x) -> p g x", x=64)
                        first = HEAD * h
                        for c in range(2):
                            ins = s.copy(to[:, :, 48 * c + first:48 * c + first + HEAD], src[:, :, c, h, :])
                ins.then_inc(s_vd, 1)

            def exponential(half, u):
                n = 2 * half + u
                act.wait_ge(s_sub, n + 1)
                s.activation(probs[:, u, :], probs[:, u, :], ACT.Exp, scale=HEAD ** -0.5).then_inc(s_exp, 1)

            def probs_copy(half, u):
                n = 2 * half + u
                act.wait_ge(s_pt, n + 1)
                used(act, s_av, n - 1)
                s.copy(probs_t[:, u, :].rearrange("p (b n) -> p b n", b=2), ps[:, 4:6, :]).then_inc(s_ptc, 1)

            def o_copy(half, u):
                n = 2 * half + u
                act.wait_ge(s_av, n + 1)
                used(act, s_pj, n - 1)
                s.copy(ot_ring[:, u, :], ps[:, 6 + u, 0:P]).then_inc(s_otc, 1)

            steps(act, TILES, [(4, probs_copy), (2, exponential), (0, spread_q), (4, spread_v), (5, o_copy)])

            def h_turn_copy(half, u):
                m = 2 * half + u
                act.wait_ge(s_htp, m + 1)
                used(act, s_lgp, m - 1)
                s.copy(ht_ring[:, u, :], ps[:, u, :]).then_inc(s_ht, 1)

            def h_high(half, u):
                m = 2 * half + u
                act.wait_ge(s_h, 4 * (m + 1))
                s.copy(h_hi[:, bass.ds(4 * m, 4), :], h_all[:, bass.ds(4 * m, 4), :]).then_inc(s_hhi, 1)

            def logits_copy(half, u):
                m = 2 * half + u
                act.wait_ge(s_lgp, m + 1)
                s.copy(logits[:, bass.ds(4 * m, 4), :],
                       ps[:, 2 + u, 0:4 * EXPERTS].rearrange("p (t e) -> p t e", t=4)).then_inc(s_lg, 1)

            steps(act, MACROS, [(0, h_high), (0, h_turn_copy), (1, logits_copy)])
            act.wait_ge(s_rt, 2)
            s.activation(rt[1][:, :, :], rt[0][:, :, :], ACT.Exp).then_inc(s_rexp, 1)

            def slots_copy(half, u):
                n = 2 * half + u
                for bank in range(2):
                    act.wait_ge(s_g[bank], n + 1)
                    s.copy(slots_at(slots_hi, n, bank),
                           ps[:, bank, 0:2 * SLOTS].rearrange("p (t s) -> p t s", t=2)).then_inc(s_gc[bank], 1)
                act.wait_ge(s_ctp, n + 1)
                s.copy(comb_t[0:HALF, :, bass.ds(n * 2 * P, 2 * P)],
                       ps[0:HALF, 4 + u, :].rearrange("p (h n) -> p h n", h=2)).then_inc(s_ctc, 1)

            steps(act, UNITS, [(0, slots_copy)])

            def high_part(q, tile, at):
                c, parity = at % CHUNKS, at // CHUNKS % 2
                act.wait_ge(s_gt, q + 1)
                if c == 0:
                    used(act, s_dn, tile - 1)
                s.copy(gated_hi[0:FC, parity, c, :], gated[0:FC, c % 2, :]).then_inc(s_ghi, 1)

            def expert(half, u):
                for i in range(PARTS * CHUNKS):
                    at = u * PARTS * CHUNKS + i
                    q = (2 * half + u) * PARTS * CHUNKS + i
                    act.wait_ge(s_h1, q + 1)
                    used(act, s_gt, q - 1)
                    s.activation(silu[0:FC, i % 2, :], ps[0:FC, at % BANKS, 0:PS], ACT.Silu).then_inc(s_si, 1)
                    if not isinstance(q, int) or q > 0:
                        tile = (2 * half + u) * PARTS + (i - 1) // CHUNKS
                        high_part(q - 1, tile, (at - 1) % PER_LOOP)

            expert(0, 0)
            expert(0, 1)
            with act.Fori(1, EXPERTS // 2) as half:
                expert(half, 0)
                expert(half, 1)
            high_part(EXPERTS * PARTS * CHUNKS - 1, EXPERTS * PARTS - 1, PER_LOOP - 1)

            def slot_copy(half, u):
                m = 2 * half + u
                for bank in range(0, 4, 2):
                    act.wait_ge(s_st[bank], m + 1)
                    used(act, s_cm, m - 1)
                    s.copy(slot_rows[0:HALF, u, 4 * bank:4 * bank + 4, :],
                           ps[0:HALF, bank, :].rearrange("p (n d) -> p n d", n=4)).then_inc(s_sr[bank], 1)

            steps(act, MACROS, [(0, slot_copy)])

        @block.vector
        def _(dve):
            v = nc.vector
            dve.wait_ge(s_const, 16 * N_CONST)
            v.tensor_scalar(bv_rows[:, :], cv["tri"], 0.0, bv_sb[:, 0:1], ALU.mult, ALU.add).then_inc(s_bvr, 1)

            def norm_stats(src, n, u, bn, mv):
                for t in range(4):
                    v.bn_stats(stats[:, u, t, :], src[:, bass.ds(4 * n + t, 1), :].rearrange("p t d -> p (t d)")
                               ).then_inc(bn, 1)
                dve.wait_ge(bn, 4 * (n + 1))
                apart(dve)
                for t in range(4):
                    v.bn_aggr(meanvar[:, u, t, :], stats[:, u, t, :]).then_inc(mv, 1)

            def ln1_stats(m):
                u = m % 2
                dve.wait_ge(s_x[m], 16)
                norm_stats(x_all, m, u, s_bn, s_mv)

            def ln1_apply(half, u):
                m = 2 * half + u
                dve.wait_ge(s_rstd, m + 1)
                used(dve, s_xnt, m - 1)
                for t in range(4):
                    v.tensor_scalar(xn_ring[:, u, t, :].unsqueeze(1), x_all[:, bass.ds(4 * m + t, 1), :],
                                    meanvar[:, u, t, 0:1], rstd[:, u, t:t + 1],
                                    ALU.subtract, ALU.mult).then_inc(s_xn, 1)

            for m in range(MACROS + 1):
                if m < MACROS:
                    used(dve, s_xn, 4 * (m - 1))
                    ln1_stats(m)
                if m == 1:
                    dve.wait_ge(s_bop, 1)
                    v.tensor_tensor(bo_sb[:, :], ps[:, 7, 0:D], bo_sb[:, :], ALU.add).then_inc(s_bo, 1)
                if m >= 1:
                    ln1_apply((m - 1) // 2, (m - 1) % 2)

            NB = 2 * GH

            def head_scores(u):
                return ps[:, 2 * u:2 * u + 2, :].rearrange("p b (h k) -> p (b h) k", k=SEQ)

            def maximum(half, u):
                n = 2 * half + u
                dve.wait_ge(s_sc, n + 1)
                v.tensor_reduce(row_max[:, u, :], head_scores(u), X, ALU.max).then_inc(s_mx, 1)

            def shift(half, u):
                n = 2 * half + u
                dve.wait_ge(s_mx, n + 1)
                used(dve, s_pt, n - 1)
                v.tensor_tensor(probs[:, u, :].rearrange("p (n k) -> p n k", k=SEQ), head_scores(u),
                                row_max[:, u, :].unsqueeze(2).to_broadcast([P, NB, SEQ]),
                                ALU.subtract).then_inc(s_sub, 1)

            def denominator(half, u):
                n = 2 * half + u
                dve.wait_ge(s_exp, n + 1)
                v.tensor_reduce(row_sum[:, u, :], probs[:, u, :].rearrange("p (n k) -> p n k", k=SEQ), X,
                                ALU.add).then_inc(s_sum, 1)
                dve.wait_ge(s_sum, n + 1)
                used(dve, s_pn, n - 1)
                v.reciprocal(rden[:, u, :], row_sum[:, u, :]).then_inc(s_rd, 1)

            def add_residual(half, u):
                n = 2 * half + u
                if isinstance(n, int) and n == 0:
                    dve.wait_ge(s_xb, MACROS)
                dve.wait_ge(s_pj, n + 1)
                v.tensor_tensor(x1_all[:, bass.ds(n, 1), :], ps[:, 6 + u, P:P + D].unsqueeze(1),
                                x1_all[:, bass.ds(n, 1), :], ALU.add).then_inc(s_x1, 1)

            steps(dve, TILES, [(5, add_residual), (0, maximum), (1, denominator), (0, shift)])

            def ln2_stats(half, u):
                n = 2 * half + u
                if isinstance(n, int) and n == 0:
                    dve.wait_ge(s_x1, TILES)
                used(dve, s_h, 4 * (n - 1))
                norm_stats(x1_all, n, u, s_bn2, s_mv2)

            def ln2_apply(half, u):
                m = 2 * half + u
                dve.wait_ge(s_rstd2, m + 1)
                for t in range(4):
                    v.tensor_scalar(h_all[:, bass.ds(4 * m + t, 1), :], x1_all[:, bass.ds(4 * m + t, 1), :],
                                    meanvar[:, u, t, 0:1], rstd[:, u, t:t + 1],
                                    ALU.subtract, ALU.mult).then_inc(s_h, 1)

            def h_low(half, u):
                m = 2 * half + u
                dve.wait_ge(s_hhi, m + 1)
                v.tensor_tensor(h_lo[:, bass.ds(4 * m, 4), :], h_all[:, bass.ds(4 * m, 4), :],
                                h_hi[:, bass.ds(4 * m, 4), :].bitcast(F32), ALU.subtract).then_inc(s_hlo, 1)

            steps(dve, MACROS, [(0, ln2_stats), (1, ln2_apply), (2, h_low)])

            done = [0]

            def then(ins):
                done[0] += 1
                ins.then_inc(s_rt, 1)
                dve.wait_ge(s_rt, done[0])

            def wide(a):
                return a[:, :].unsqueeze(2).to_broadcast([P, TILES, EXPERTS])

            rank = cv["rank"].unsqueeze(1).to_broadcast([P, TILES, EXPERTS])
            dve.wait_ge(s_lg, MACROS)
            then(v.tensor_reduce(rs[0][:, :], logits[:, :, :], X, ALU.max))
            then(v.tensor_tensor(rt[0][:, :, :], logits[:, :, :], wide(rs[0]), ALU.subtract))
            dve.wait_ge(s_rexp, 1)
            then(v.tensor_reduce(rs[1][:, :], rt[1][:, :, :], X, ALU.add))
            then(v.reciprocal(rs[2][:, :], rs[1][:, :]))
            then(v.tensor_tensor(prob[:, :, :], rt[1][:, :, :], wide(rs[2]), ALU.mult))

            def first_largest(values, largest, equal, weighted, best, chosen):
                then(v.tensor_reduce(largest[:, :], values[:, :, :], X, ALU.max))
                then(v.tensor_tensor(equal[:, :, :], values[:, :, :], wide(largest), ALU.is_equal))
                then(v.tensor_tensor(weighted[:, :, :], equal[:, :, :], rank, ALU.mult))
                then(v.tensor_reduce(best[:, :], weighted[:, :, :], X, ALU.max))
                then(v.tensor_tensor(chosen[:, :, :], weighted[:, :, :], wide(best), ALU.is_equal))

            first_largest(prob, rs[3], rt[2], rt[3], rs[4], rt[4])
            then(v.scalar_tensor_tensor(out=rt[5][:, :, :], in0=rt[4][:, :, :], scalar=-2.0, in1=prob[:, :, :],
                                        op0=ALU.mult, op1=ALU.add))
            first_largest(rt[5], rs[5], rt[2], rt[3], rs[0], rt[6])
            then(v.tensor_tensor(rt[7][:, :, :], rt[4][:, :, :], rt[6][:, :, :], ALU.add))
            dve.wait_ge(s_pos, 1)
            then(v.tensor_tensor(places[:, :, :], ps[:, 5, 0:TILES * EXPERTS].rearrange("p (t e) -> p t e", e=EXPERTS),
                                 rt[7][:, :, :], ALU.mult))

            def one_hot(half, u):
                n = 2 * half + u
                used(dve, s_g[2], n - 1)
                used(dve, s_g[3], n - 1)
                used(dve, s_cb, n - 1)
                v.tensor_tensor(onehot[:, u, :, :].rearrange("p t (e c) -> p (t e) c", e=EXPERTS),
                                places[:, bass.ds(2 * n, 2), :].rearrange("p t e -> p (t e)").unsqueeze(2)
                                .to_broadcast([P, 2 * EXPERTS, CAP]),
                                cv["place"].unsqueeze(1).to_broadcast([P, 2 * EXPERTS, CAP]),
                                ALU.is_equal).then_inc(s_oh, 1)

            def slots_copy(half, u):
                n = 2 * half + u
                for bank in range(2):
                    dve.wait_ge(s_g[2 + bank], n + 1)
                    v.tensor_copy(slots_at(slots_lo, n, bank),
                                  ps[:, 2 + bank, 0:2 * SLOTS].rearrange("p (t s) -> p t s", t=2)
                                  ).then_inc(s_gc[2 + bank], 1)

            steps(dve, UNITS, [(0, one_hot), (1, slots_copy)])

            def expert_out_copy(tile, e, part, parity):
                dve.wait_ge(s_dn, tile + 1)
                v.tensor_copy(expert_slots(expert_out, e, part),
                              ps[:, 6 + parity, 0:PS].rearrange("p (b c) -> p b c", c=CAP)).then_inc(s_eo, 1)

            def low_part(q, tile, at):
                c, parity = at % CHUNKS, at // CHUNKS % 2
                dve.wait_ge(s_ghi, q + 1)
                if c == 0:
                    used(dve, s_dn, tile - 1)
                v.tensor_tensor(gated_lo[0:FC, parity, c, :], gated[0:FC, c % 2, :],
                                gated_hi[0:FC, parity, c, :].bitcast(F32), ALU.subtract).then_inc(s_glo, 1)

            def expert(half, u):
                e = 2 * half + u
                for i in range(PARTS * CHUNKS):
                    at = u * PARTS * CHUNKS + i
                    q = e * PARTS * CHUNKS + i
                    dve.wait_ge(s_h3, q + 1)
                    dve.wait_ge(s_si, q + 1)
                    used(dve, s_ghi, q - 1)
                    used(dve, s_glo, q - 1)
                    v.tensor_tensor(gated[0:FC, i % 2, :], ps[0:FC, BANKS + at % BANKS, 0:PS], silu[0:FC, i % 2, :],
                                    ALU.mult).then_inc(s_gt, 1)
                    tile = e * PARTS + i // CHUNKS
                    if not isinstance(q, int) or q > 0:
                        low_part(q - 1, e * PARTS + (i - 1) // CHUNKS, (at - 1) % PER_LOOP)
                    if i % CHUNKS == 3 and (not isinstance(tile, int) or tile > 0):
                        part = i // CHUNKS
                        expert_out_copy(tile - 1, e if part else e - 1, (part - 1) % PARTS, (part - 1) % 2)

            for i in range(4):
                dve.wait_ge(s_g[i], UNITS)
            expert(0, 0)
            expert(0, 1)
            with dve.Fori(1, EXPERTS // 2) as half:
                expert(half, 0)
                expert(half, 1)
            low_part(EXPERTS * PARTS * CHUNKS - 1, EXPERTS * PARTS - 1, PER_LOOP - 1)
            expert_out_copy(EXPERTS * PARTS - 1, EXPERTS - 1, PARTS - 1, (PARTS - 1) % 2)

            def slot_copy(half, u):
                m = 2 * half + u
                for bank in range(1, 4, 2):
                    dve.wait_ge(s_st[bank], m + 1)
                    used(dve, s_cm, m - 1)
                    v.tensor_copy(slot_rows[0:HALF, u, 4 * bank:4 * bank + 4, :],
                                  ps[0:HALF, bank, :].rearrange("p (n d) -> p n d", n=4)).then_inc(s_sr[bank], 1)

            def add_experts(half, u):
                m = 2 * half + u
                dve.wait_ge(s_cm, m + 1)
                used(dve, s_os[u], 16 * half)
                v.tensor_tensor(out_ring[:, u, :, :], ps[:, 4 + u, :].rearrange("p (t d) -> p t d", t=4),
                                x1_all[:, bass.ds(4 * m, 4), :], ALU.add).then_inc(s_oc, 1)

            steps(dve, MACROS, [(0, slot_copy), (1, add_experts)])

        @block.tensor
        def _(pe):
            mm = nc.tensor.matmul
            turn = nc.tensor.transpose
            pe.wait_ge(s_const, 16 * N_CONST)
            pe.wait_ge(s_bvr, 1)
            mm(ps[:, 7, 0:D], bv_rows[:, :], wo_sb[:, :], start=True, stop=True).then_inc(s_bop, 1)

            def project(half, u):
                m = 2 * half + u
                pe.wait_ge(s_ctx[u], 16 * (half + 1))
                used(pe, s_k, m)
                mm(ps[:, 2, :], wk_sb[:, :], ctx_ring[:, u, :], start=True, stop=True).then_inc(s_kp, 1)
                used(pe, s_v, m)
                for t in range(4):
                    ins = mm(ps[:, 3, t * D:(t + 1) * D], ctx_ring[:, u, t * P:(t + 1) * P], wv_sb[:, :],
                             start=True, stop=True)
                ins.then_inc(s_vp, 1)
                pe.wait_ge(s_xn, 4 * (m + 1))
                used(pe, s_xntc, m)
                for t in range(4):
                    ins = turn(ps[:, 0, t * P:(t + 1) * P], xn_ring[:, u, t, :], ident)
                ins.then_inc(s_xnt, 1)

            def project_q(half, u):
                m = 2 * half + u
                pe.wait_ge(s_xntc, m + 1)
                used(pe, s_q, m)
                mm(ps[:, 1, :], wq_sb[:, :], xnt_ring[:, u, :], start=True, stop=True).then_inc(s_qp, 1)

            steps(pe, MACROS, [(0, project), (1, project_q)])

            def scores(half, u):
                n = 2 * half + u
                if isinstance(n, int) and n == 0:
                    pe.wait_ge(s_q, MACROS)
                    pe.wait_ge(s_v, MACROS)
                pe.wait_ge(s_qd, n + 1)
                pe.wait_ge(s_kd, n + 1)
                used(pe, s_sub, n - 1)
                for b in range(2):
                    ins = mm(ps[:, 2 * u + b, :], q_diag[:, u, b, :], k_diag[:, u, b, :, :], start=True, stop=True)
                ins.then_inc(s_sc, 1)

            def turn_probs(half, u):
                n = 2 * half + u
                pe.wait_ge(s_pn, n + 1)
                used(pe, s_ptc, n)
                for i in range(2 * PAIRS):
                    ins = turn(ps[:, 4 + i // 4, (i % 4) * P:(i % 4 + 1) * P], probs[:, u, i * P:(i + 1) * P], ident)
                ins.then_inc(s_pt, 1)

            def weigh(half, u):
                n = 2 * half + u
                pe.wait_ge(s_vd, n + 1)
                pe.wait_ge(s_ptc, n + 1)
                used(pe, s_x1, n - 1)
                for b in range(2):
                    for g in range(GROUPS):
                        for c in range(PAIRS):
                            rows = 32 * (2 * g + c // 2)
                            src = (b * PAIRS + c) * P + g * SEQ
                            ins = mm(ps[rows:rows + 32, 6 + u, b * SEQ:(b + 1) * SEQ], v_diag[:, u, b, g, c, :],
                                     probs_t[:, u, src:src + SEQ], start=(c % 2 == 0), stop=(c % 2 == 1))
                ins.then_inc(s_av, 1)

            def out_product(half, u):
                n = 2 * half + u
                pe.wait_ge(s_otc, n + 1)
                mm(ps[:, 6 + u, P:P + D], ot_ring[:, u, :], wo_sb[:, :], start=True, stop=True).then_inc(s_pj, 1)

            steps(pe, TILES, [(0, scores), (2, turn_probs), (3, weigh), (4, out_product)])

            def h_turn(m):
                pe.wait_ge(s_h, 4 * (m + 1))
                used(pe, s_ht, m - 1)
                for t in range(4):
                    ins = turn(ps[:, m % 2, t * P:(t + 1) * P], h_all[:, 4 * m + t, :], ident)
                ins.then_inc(s_htp, 1)

            def route(m):
                pe.wait_ge(s_ht, m + 1)
                used(pe, s_lg, m - 1)
                for t in range(4):
                    ins = mm(ps[:, 2 + m % 2, t * EXPERTS:(t + 1) * EXPERTS], ht_ring[:, m % 2, t * P:(t + 1) * P],
                             gate_sb[:, :], start=True, stop=True)
                ins.then_inc(s_lgp, 1)

            for m in range(MACROS + 1):
                if m < MACROS:
                    h_turn(m)
                if m >= 1:
                    route(m - 1)

            pe.wait_ge(s_rt, 17)
            mm(ps[:, 5, 0:TILES * EXPERTS], cv["tri"], rt[7][:, :, :], start=True, stop=True).then_inc(s_pos, 1)

            def gather(n):
                u = n % 2
                pe.wait_ge(s_oh, n + 1)
                for lo in range(2):
                    if n == 0:
                        pe.wait_ge(s_hlo if lo else s_hhi, MACROS)
                    part = h_lo if lo else h_hi
                    for odd in range(2):
                        used(pe, s_gc[2 * lo + odd], n)
                    for t in range(2):
                        for odd in range(2):
                            rows = slice(odd * SEQ, (odd + 1) * SEQ)
                            ins = mm(ps[:, 2 * lo + odd, t * SLOTS:(t + 1) * SLOTS], part[rows, 2 * n + t, :],
                                     onehot[rows, u, t, :], start=True, stop=True)
                            if t:
                                ins.then_inc(s_g[2 * lo + odd], 1)

            def turn_comb(n):
                u = n % 2
                pe.wait_ge(s_cb, n + 1)
                used(pe, s_ctc, n - 1)
                if n == 1:
                    pe.wait_ge(s_rt, 18)
                for h in range(2):
                    for t in range(2):
                        ins = turn(ps[0:HALF, 4 + u, (2 * h + t) * P:(2 * h + t + 1) * P],
                                   comb[:, u, t, h * HALF:(h + 1) * HALF], ident)
                ins.then_inc(s_ctp, 1)

            for n in range(UNITS + 1):
                if n < UNITS:
                    gather(n)
                if n >= 1:
                    turn_comb(n - 1)

            def up(e, part, u):
                for c in range(CHUNKS):
                    at = (u * PARTS + part) * CHUNKS + c
                    q = (e * PARTS + part) * CHUNKS + c
                    cols = slice(c * FC, (c + 1) * FC)
                    hi, lo = expert_slots(slots_hi, e, part), expert_slots(slots_lo, e, part)
                    for w, free, done in ((0, s_si, s_h1), (1, s_gt, s_h3)):
                        used(pe, free, q - before(at) + 1)
                        bank = ps[0:FC, BANKS * w + at % BANKS, 0:PS]
                        mm(bank, w13_lo[:, u, w, cols], hi, start=True, stop=False)
                        mm(bank, w13_hi[:, u, w, cols], lo, start=False, stop=False)
                        mm(bank, w13_hi[:, u, w, cols], hi, start=False, stop=True).then_inc(done, 1)

            def down(tile, part, u):
                used(pe, s_eo, tile - 1)
                bank = ps[:, 6 + part % 2, 0:PS]
                for c in range(CHUNKS):
                    pe.wait_ge(s_ghi, tile * CHUNKS + c + 1)
                    mm(bank, w2_lo[0:FC, u, c, :], gated_hi[0:FC, part % 2, c, :], start=(c == 0), stop=False)
                    mm(bank, w2_hi[0:FC, u, c, :], gated_hi[0:FC, part % 2, c, :], start=False, stop=False)
                    pe.wait_ge(s_glo, tile * CHUNKS + c + 1)
                    ins = mm(bank, w2_hi[0:FC, u, c, :], gated_lo[0:FC, part % 2, c, :], start=False,
                             stop=(c == CHUNKS - 1))
                ins.then_inc(s_dn, 1)

            def expert(half, u):
                e = 2 * half + u
                pe.wait_ge(s_wlo, 2 * (e + 1))
                for part in range(PARTS):
                    tile = e * PARTS + part
                    up(e, part, u)
                    if not isinstance(tile, int) or tile > 0:
                        down(tile - 1, (part - 1) % PARTS, u if part else 1 - u)

            pe.wait_ge(s_ctc, UNITS)
            for i in range(4):
                pe.wait_ge(s_gc[i], UNITS)
            expert(0, 0)
            expert(0, 1)
            with pe.Fori(1, EXPERTS // 2) as half:
                expert(half, 0)
                expert(half, 1)
            down(EXPERTS * PARTS - 1, PARTS - 1, 1)

            def turn_slots(m):
                for bank in range(4):
                    used(pe, s_sr[bank], m)
                    for i in range(4):
                        ins = turn(ps[0:HALF, bank, i * D:(i + 1) * D],
                                   expert_out[:, (16 * m + 4 * bank + i) * HALF:(16 * m + 4 * bank + i + 1) * HALF], ident)
                    ins.then_inc(s_st[bank], 1)

            def combine(m):
                used(pe, s_oc, m - 1)
                for b in range(8):
                    if b % 2 == 0:
                        pe.wait_ge(s_sr[b // 2], m + 1)
                    rows = slice(b % 2 * SEQ, (b % 2 + 1) * SEQ)
                    for h in range(2):
                        ins = mm(ps[rows, 4 + m % 2, b // 2 * D:(b // 2 + 1) * D],
                                 comb_t[0:HALF, h, m * MT + b * SEQ:m * MT + (b + 1) * SEQ],
                                 slot_rows[0:HALF, m % 2, 2 * b + h, :], start=(h == 0), stop=(h == 1))
                ins.then_inc(s_cm, 1)

            pe.wait_ge(s_eo, EXPERTS * PARTS)
            for m in range(MACROS + 1):
                if m < MACROS:
                    turn_slots(m)
                if m >= 1:
                    combine(m - 1)


def kernel(**inputs):
    import numpy as _np
    import concourse.bacc as _bacc
    from concourse import mybir as _mybir
    from concourse.bass_utils import run_bass_kernel_spmd as _run

    def laid(name):
        return _np.asarray(inputs[name])

    def weight(name):
        return _np.ascontiguousarray(laid(name).T)

    def column(name):
        return _np.ascontiguousarray(laid(name).reshape(-1, 1))

    arrays = {
        "x": laid("x").reshape(TOKENS, D),
        "ctx_t": _np.ascontiguousarray(laid("ctx_1024").reshape(TOKENS, D).T),
        "consts": constants(),
        "wq": weight("L0_xattn_Wq"),
        "wk": weight("L0_xattn_Wk"),
        "wv": weight("L0_xattn_Wv"),
        "wo": weight("L0_xattn_Wo"),
        "bq": column("L0_xattn_bq"),
        "bk": column("L0_xattn_bk"),
        "bv": column("L0_xattn_bv"),
        "bo": _np.ascontiguousarray(_np.broadcast_to(laid("L0_xattn_bo"), (P, D))),
        "gate": weight("L0_ffn_gate_w"),
        "w1": _np.ascontiguousarray(laid("L0_ffn_w1").transpose(1, 0, 2).reshape(D, EXPERTS * FFN)),
        "w2": _np.ascontiguousarray(
            laid("L0_ffn_w2").reshape(EXPERTS * CHUNKS, FC, D).transpose(1, 0, 2)),
        "w3": _np.ascontiguousarray(laid("L0_ffn_w3").transpose(1, 0, 2).reshape(D, EXPERTS * FFN)),
    }
    nc = _bacc.Bacc("TRN2", target_bir_lowering=False, num_devices=1)
    args = [nc.dram_tensor(f"in_{n}", a.shape, _mybir.dt.from_np(a.dtype), kind="ExternalInput").ap()
            for n, a in arrays.items()]
    out = nc.dram_tensor("out", (TOKENS, D), _mybir.dt.float32, kind="ExternalOutput").ap()
    build(nc, *args, out)
    r = _run(nc, [{f"in_{n}": a for n, a in arrays.items()}], core_ids=[0])
    return r.results[0]["out"].reshape(SEQS, SEQ, D)
```

```python
from contextlib import ExitStack

import numpy as np

import concourse.bass as bass
from concourse import mybir

ALU = mybir.AluOpType
ACT = mybir.ActivationFunctionType
F32 = mybir.dt.float32
F32R = mybir.dt.float32r
X = mybir.AxisListType.X

SEQS, SEQ, D = 64, 64, 128
HEADS = 16
HEAD = D // HEADS
EXPERTS, TOPK, FFN = 8, 2, 448
CAP = int(SEQ * TOPK / EXPERTS * 1.25)
EPS = 1e-5

P = 128
TOKENS = SEQS * SEQ
TILES = TOKENS // P
MACROS = TILES // 4
UNITS = TILES // 2
MT = 4 * P
LED = MACROS - 2
GROUPS = 2
GH = HEADS // GROUPS
PAIRS = GH // 2
SLOTS = EXPERTS * CAP
HALF = SLOTS // 2
ESLOTS = SEQS * CAP
PARTS = 4
PS = ESLOTS // PARTS
CHUNKS = 4
LAST = CHUNKS - 1
REST = FFN - LAST * P
assert 2 * REST == P
EARLY = dict(wk=D, wv=D, bk=1, bq=1, ident=P)
LATE = dict(wq=D, wo=D, bv=1, bo=D, gate=EXPERTS, tri=P, headmask=GH, place=CAP, rank=EXPERTS)


def constants():
    p = np.arange(P)
    return dict(
        ident=np.eye(P, dtype=np.float32),
        tri=((p[:, None] // SEQ == p[None, :] // SEQ) & (p[:, None] <= p[None, :])).astype(np.float32),
        headmask=((p[:, None] % (GH * HEAD)) // HEAD == np.arange(GH)[None, :]).astype(np.float32),
        place=np.tile(np.arange(1, CAP + 1, dtype=np.float32), (P, 1)),
        rank=np.tile(np.arange(EXPERTS, 0, -1, dtype=np.float32), (P, 1)),
    )


def used(eng, semaphore, count):
    if not isinstance(count, int) or count > 0:
        eng.wait_ge(semaphore, count)


def steps(eng, n, stages, lead=None, drain=None):
    depth = max(lag for lag, _ in stages)
    head = (depth + 3) // 2

    def slot(pair, u):
        for lag, stage in stages:
            parity = (u - lag) % 2
            half = pair + (u - lag - parity) // 2
            if isinstance(pair, int) and not 0 <= 2 * half + parity < n:
                continue
            stage(half, parity)

    for pair in range(min(head, n // 2)):
        for u in range(2):
            if lead:
                lead(2 * pair + u)
            slot(pair, u)
    if head < n // 2:
        with eng.Fori(head, n // 2) as pair:
            slot(pair, 0)
            slot(pair, 1)
    for t in range(n, n + depth):
        slot(t // 2, t % 2)
        if drain:
            drain(t - n)


def build(nc, x, ctx_t, early, late, w13, w2, out):
    with ExitStack() as stack:
        def sem(name):
            return stack.enter_context(nc.semaphore(name))

        ARENA = 212000
        arena = -(-nc.sbuf_base // 64) * 64
        stack.enter_context(nc.sbuf_tensor("arena", [P, ARENA], mybir.dt.uint8, align_bytes=64))
        top = {}

        def region(name, at):
            top[name] = at
            return name

        def place(name_of_region, name, shape, dtype=F32):
            at = -(-top[name_of_region] // 32) * 32
            top[name_of_region] = at + 4 * int(np.prod(shape[1:]))
            assert top[name_of_region] <= ARENA, name
            return nc.alloc_sbuf_tensor_at(name, shape, dtype, offset=arena + at)

        A = region("attention_inputs", 0)
        q_all = place(A, "q_all", [P, TOKENS])
        k_all = place(A, "k_all", [P, TOKENS])
        v_all = place(A, "v_all", [P, TILES, D])
        x_all = place(A, "x_all", [P, TILES, D])
        A2 = region("slots", 0)
        slots_hi = place(A2, "slots_hi", [P, SEQS * SLOTS], F32R)
        slots_lo = place(A2, "slots_lo", [P, SEQS * SLOTS], F32R)
        A3 = region("outputs", 0)
        expert_out = place(A3, "expert_out", [P, SEQS * SLOTS])
        slot_rows = place(A3, "slot_rows", [P, 2, 16, D])
        out_ring = place(A3, "out_ring", [P, 2, 4, D])
        A4 = region("router", 0)
        h_all = place(A4, "h_all", [P, TILES, D])
        ht_ring = place(A4, "ht_ring", [P, 2, MT])
        logits = place(A4, "logits", [P, TILES, EXPERTS])
        rt = [place(A4, f"route_{i}", [P, TILES, EXPERTS]) for i in range(8)]
        rs = [place(A4, f"route_s{i}", [P, TILES]) for i in range(6)]

        B = region("residual", top[A2])
        x1_all = place(B, "x1_all", [P, TILES, D])
        C = region("combine_weights", top[B])
        comb_t = place(C, "comb_t", [P, 2, TOKENS])
        C2 = region("attention_rings", top[B])
        q_diag = place(C2, "q_diag", [P, 2, 2, P])
        k_diag = place(C2, "k_diag", [P, 2, 2, GH, SEQ])
        probs = place(C2, "probs", [P, 2, 2 * GH * SEQ])
        probs_t = place(C2, "probs_t", [P, 2, 2 * PAIRS * P])
        v_diag = place(C2, "v_diag", [P, 2, 2, GROUPS, PAIRS, 32])
        ot_ring = place(C2, "ot_ring", [P, 2, P])
        row_max = place(C2, "row_max", [P, 2, 2 * GH])
        row_sum = place(C2, "row_sum", [P, 2, 2 * GH])
        rden = place(C2, "rden", [P, 2, 2 * GH])
        DD = region("h_parts", top[C])
        h_hi = place(DD, "h_hi", [P, TILES, D], F32R)
        h_lo = place(DD, "h_lo", [P, TILES, D], F32R)
        D1 = region("projection_rings", top[C])
        ctx_ring = place(D1, "ctx_ring", [P, 2, MT])
        xn_ring = place(D1, "xn_ring", [P, 2, 4, D])
        xnt_ring = place(D1, "xnt_ring", [P, 2, MT])
        bv_rows = place(D1, "bv_rows", [P, D])
        D2 = region("gated_values", top[C])
        silu = place(D2, "silu", [P, 2, PS])
        gated = place(D2, "gated", [P, 2, PS])
        gated_hi = place(D2, "gated_hi", [P, 2, CHUNKS, PS], F32R)
        gated_lo = place(D2, "gated_lo", [P, 2, CHUNKS, PS], F32R)
        W = region("weights", top[DD])
        w13_raw = place(W, "w13_raw", [P, 2, 2 * FFN])
        w2_raw = place(W, "w2_raw", [P, 2, CHUNKS, D])
        w13_hi = place(W, "w13_hi", [P, 2, 2 * FFN], F32R)
        w13_lo = place(W, "w13_lo", [P, 2, 2 * FFN], F32R)
        w2_hi = place(W, "w2_hi", [P, 2, CHUNKS, D], F32R)
        w2_lo = place(W, "w2_lo", [P, 2, CHUNKS, D], F32R)
        K = region("kept", top[W])
        early_sb = place(K, "early_sb", [P, sum(EARLY.values())])
        late_sb = place(K, "late_sb", [P, sum(LATE.values())])
        half_neg = place(K, "half_neg", [P, 4])
        meanvar2 = place(K, "meanvar2", [P, TILES, 2])
        rstd2 = place(K, "rstd2", [P, TILES])
        stats = place(K, "stats", [P, 2, 4, 6])
        meanvar = place(K, "meanvar", [P, 2, 4, 2])
        var_eps = place(K, "var_eps", [P, 2, 4])
        rstd = place(K, "rstd", [P, 2, 4])
        prob = place(K, "prob", [P, TILES, EXPERTS])
        places = place(K, "places", [P, TILES, EXPERTS])
        onehot = place(K, "onehot", [P, 2, 2, 2, SLOTS], F32R)
        comb = place(K, "comb", [P, 2, 2, SLOTS])

        cv = {}
        for buffer, columns in ((early_sb, EARLY), (late_sb, LATE)):
            at = 0
            for name, cols in columns.items():
                cv[name] = buffer[:, at:at + cols]
                at += cols
        ident, wq_sb, wk_sb, wv_sb, wo_sb, gate_sb, bq_sb, bk_sb, bv_sb, bo_sb = (
            cv[n] for n in ("ident", "wq", "wk", "wv", "wo", "gate", "bq", "bk", "bv", "bo"))

        ps = stack.enter_context(nc.psum_tensor("ps", [P, 8, 512], F32))

        s_apart = sem("wait_carrier")
        s_early = sem("early_constants_in")
        s_late = sem("late_constants_in")
        s_x = [sem(f"x_in{m}") for m in range(MACROS)]
        s_ctx = [sem(f"ctx_in{u}") for u in range(2)]
        s_w = [sem(f"weights_in{u}") for u in range(2)]
        s_zero = sem("diagonals_cleared")
        s_hneg = sem("half_neg_set")
        s_bvr = sem("bv_rows_ready")
        s_bop = sem("bo_product")
        s_bo = sem("bo_ready")
        s_bn = sem("stats_taken")
        s_mv = sem("meanvar_ready")
        s_ve = sem("var_eps_ready")
        s_rstd = sem("rstd_ready")
        s_xn = sem("xn_ready")
        s_xb = sem("residual_ready")
        s_xnt = sem("xnt_product")
        s_xntc = sem("xnt_ready")
        s_kp = sem("k_product")
        s_vp = sem("v_product")
        s_qp = sem("q_product")
        s_k = sem("k_ready")
        s_v = sem("v_ready")
        s_q = sem("q_ready")
        s_kd = sem("k_diag_ready")
        s_qd = sem("q_diag_ready")
        s_vd = sem("v_diag_ready")
        s_sc = sem("scores_done")
        s_mx = sem("row_max_ready")
        s_sub = sem("shifted_ready")
        s_exp = sem("exp_ready")
        s_sum = sem("row_sum_ready")
        s_rd = sem("rden_ready")
        s_pn = sem("probs_ready")
        s_pt = sem("probs_turned")
        s_ptc = sem("probs_t_ready")
        s_av = sem("pv_done")
        s_otc = sem("ot_ready")
        s_pj = sem("out_product")
        s_x1 = sem("x1_ready")
        s_bn2 = sem("stats2_taken")
        s_mvt = sem("tile_meanvar_ready")
        s_mv2 = sem("meanvar2_ready")
        s_ve2 = sem("var_eps2_ready")
        s_rstd2 = sem("rstd2_ready")
        s_h = sem("h_ready")
        s_htp = sem("ht_product")
        s_ht = sem("ht_ready")
        s_lgp = sem("logits_product")
        s_lg = sem("logits_ready")
        s_rt = sem("route_step")
        s_rsh = sem("route_shifted")
        s_ch = sem("chosen_ready")
        s_pl = sem("places_ready")
        s_rexp = sem("route_exp")
        s_pos = sem("place_product")
        s_hhi = sem("h_hi_ready")
        s_hlo = sem("h_lo_ready")
        s_oh = sem("onehot_ready")
        s_cb = sem("comb_ready")
        s_g = [sem(f"gather_product{i}") for i in range(4)]
        s_gc = [sem(f"slots_ready{i}") for i in range(4)]
        s_ctp = sem("comb_turned")
        s_ctc = sem("comb_t_ready")
        s_whi = sem("weights_hi_ready")
        s_wlo = sem("weights_lo_ready")
        s_h1 = sem("up1_done")
        s_h3 = sem("up3_done")
        s_si = sem("silu_ready")
        s_gt = sem("gated_ready")
        s_ghi = sem("gated_hi_ready")
        s_glo = sem("gated_lo_ready")
        s_dn = sem("down_done")
        s_eo = sem("expert_out_ready")
        s_st = [sem(f"slots_turned{i}") for i in range(4)]
        s_sr = [sem(f"slot_rows_ready{i}") for i in range(4)]
        s_cm = sem("combine_done")
        s_oc = sem("out_ready")
        s_os = [sem(f"out_stored{u}") for u in range(2)]

        def apart(eng):
            eng.sem_inc(s_apart, 1)

        def slots_at(slots, tile):
            return slots[:, bass.ds(tile * 2 * SLOTS, 2 * SLOTS)]

        def expert_slots(slots, e, part):
            seqs = SEQS // PARTS
            return slots[:, :].rearrange("p (b s) -> p b s", b=SEQS)[
                :, part * seqs:(part + 1) * seqs, bass.ds(e * CAP, CAP)]

        UP, BOTH, DOWN = (0, LAST), 2 * LAST, 2 * LAST + 1
        LOWER, UPPER = slice(0, REST), slice(REST, P)

        block = stack.enter_context(nc.Block())

        @block.sync
        def _(sp):
            x_v = x.rearrange("(t p) d -> p t d", p=P)
            sp.dma_start(early_sb[:, :], early).then_inc(s_early, 16)

            def load_ctx(half, u):
                used(sp, s_vp, 2 * half + u - 1)
                sp.dma_start(ctx_ring[:, u, :], ctx_t[:, bass.ds((2 * half + u) * MT, MT)]).then_inc(s_ctx[u], 16)

            load_ctx(0, 0)
            sp.dma_start(x_all[:, 0:4, :], x_v[:, 0:4, :]).then_inc(s_x[0], 16)
            sp.dma_start(late_sb[:, :], late).then_inc(s_late, 16)
            load_ctx(0, 1)
            for m in range(1, MACROS):
                sp.dma_start(x_all[:, 4 * m:4 * m + 4, :], x_v[:, 4 * m:4 * m + 4, :]).then_inc(s_x[m], 16)
            with sp.Fori(1, MACROS // 2) as half:
                load_ctx(half, 0)
                load_ctx(half, 1)

            def load_weights(half, u):
                used(sp, s_wlo, 2 * (2 * half + u - 1))
                e = 2 * half + u
                sp.dma_start(w13_raw[:, u, :], w13[:, bass.ds(e * 2 * FFN, 2 * FFN)]).then_inc(s_w[u], 16)
                sp.dma_start(w2_raw[:, u, :, :], w2[:, bass.ds(e * CHUNKS, CHUNKS), :]).then_inc(s_w[u], 16)

            load_weights(0, 0)
            load_weights(0, 1)
            with sp.Fori(1, EXPERTS // 2) as half:
                load_weights(half, 0)
                load_weights(half, 1)

            out_v = out.rearrange("(t p) d -> p t d", p=P)

            def store(half, u):
                m = 2 * half + u
                sp.wait_ge(s_oc, m + 1)
                sp.dma_start(out_v[:, bass.ds(4 * m, 4), :], out_ring[:, u, :, :]).then_inc(s_os[u], 16)

            store(0, 0)
            store(0, 1)
            with sp.Fori(1, MACROS // 2) as half:
                store(half, 0)
                store(half, 1)
            for u in range(2):
                sp.wait_ge(s_os[u], 16 * MACROS // 2)

        @block.gpsimd
        def _(pool):
            g = nc.gpsimd
            g.memset(half_neg[:, :], -0.5).then_inc(s_hneg, 1)
            pool.wait_ge(s_hneg, 1)

            def ln1(half, u):
                n = 2 * half + u
                used(pool, s_xn, 4 * (n - 1))
                pool.wait_ge(s_mv, 4 * (n + 1))
                apart(pool)
                g.tensor_scalar(var_eps[:, u, :], meanvar[:, u, :, 1], EPS, None, ALU.add).then_inc(s_ve, 1)
                pool.wait_ge(s_ve, n + 1)
                g.tensor_tensor(rstd[:, u, :], var_eps[:, u, :], half_neg[:, :], ALU.pow).then_inc(s_rstd, 1)

            def clear_diagonals():
                g.memset(q_diag[:, :, :, :], 0.0).then_inc(s_zero, 1)
                g.memset(v_diag[:, :, :, :, :, :], 0.0).then_inc(s_zero, 1)
                g.memset(onehot[:, :, :, :, :].bitcast(F32), 0.0).then_inc(s_zero, 1)

            def residual(half, u):
                m = 2 * half + u
                g.tensor_tensor(x1_all[:, bass.ds(4 * m, 4), :], x_all[:, bass.ds(4 * m, 4), :],
                                bo_sb.unsqueeze(1).to_broadcast([P, 4, D]), ALU.add).then_inc(s_xb, 1)

            ln1(0, 0)
            clear_diagonals()
            ln1(0, 1)
            pool.wait_ge(s_bo, 1)
            with pool.Fori(1, MACROS // 2) as half:
                residual(half - 1, 0)
                residual(half - 1, 1)
                ln1(half, 0)
                ln1(half, 1)

            def spread_k(half, u):
                s = 2 * half + u
                if isinstance(s, int) and s % 4 == 0:
                    pool.wait_ge(s_k, 1 if s == 0 else MACROS)
                used(pool, s_sc, s - 1)
                g.tensor_tensor(k_diag[:, u, :, :, :],
                                k_all[:, bass.ds(s * P, P)].rearrange("p (b k) -> p b k", b=2).unsqueeze(2)
                                .to_broadcast([P, 2, GH, SEQ]),
                                cv["headmask"].unsqueeze(1).unsqueeze(3).to_broadcast([P, 2, GH, SEQ]),
                                ALU.mult).then_inc(s_kd, 1)

            def normalise(half, u):
                n = 2 * half + u
                pool.wait_ge(s_rd, n + 1)
                e = probs[:, u, :].rearrange("p (n k) -> p n k", k=SEQ)
                g.tensor_tensor(e, e, rden[:, u, :].unsqueeze(2).to_broadcast([P, 2 * GH, SEQ]),
                                ALU.mult).then_inc(s_pn, 1)

            def keep_meanvar(half, u):
                n = 2 * half + u
                pool.wait_ge(s_mvt, n + 1)
                apart(pool)
                g.tensor_copy(meanvar2[:, bass.ds(n, 1), :], meanvar[:, u, 0:1, :]).then_inc(s_mv2, 1)

            def ln2_rstd(m):
                tiles = slice(4 * m, 4 * m + 4)
                pool.wait_ge(s_mv2, 4 * (m + 1))
                g.tensor_scalar(rstd2[:, tiles], meanvar2[:, tiles, 1], EPS, None, ALU.add).then_inc(s_ve2, 1)
                pool.wait_ge(s_ve2, m + 1)
                g.tensor_tensor(rstd2[:, tiles], rstd2[:, tiles], half_neg[:, :], ALU.pow).then_inc(s_rstd2, 1)

            def last_residuals(t):
                if 2 <= t < 4:
                    residual(MACROS // 2 - 1, t - 2)

            steps(pool, TILES, [(0, spread_k), (3, normalise), (9, keep_meanvar)], lead=last_residuals,
                  drain=lambda m: ln2_rstd(m) if m < MACROS - 1 else None)
            ln2_rstd(MACROS - 1)

            def split_weights(half, u):
                e = 2 * half + u
                pool.wait_ge(s_w[u], 32 * (half + 1))
                used(pool, s_dn, PARTS * (e - 1))
                apart(pool)
                g.tensor_copy(w13_hi[:, u, :], w13_raw[:, u, :]).then_inc(s_whi, 1)
                g.tensor_copy(w2_hi[:, u, :, :], w2_raw[:, u, :, :]).then_inc(s_whi, 1)
                pool.wait_ge(s_whi, 2 * (e + 1))
                g.tensor_tensor(w13_lo[:, u, :], w13_raw[:, u, :], w13_hi[:, u, :],
                                ALU.subtract).then_inc(s_wlo, 1)
                g.tensor_tensor(w2_lo[:, u, :, :], w2_raw[:, u, :, :], w2_hi[:, u, :, :],
                                ALU.subtract).then_inc(s_wlo, 1)

            split_weights(0, 0)
            split_weights(0, 1)

            def weigh_onehot(half, u):
                n = 2 * half + u
                pool.wait_ge(s_oh, n + 1)
                used(pool, s_ctp, n - 1)
                for b in range(2):
                    rows = slice(b * SEQ, (b + 1) * SEQ)
                    g.tensor_tensor(
                        comb[rows, u, :, :].rearrange("p t (e c) -> p t e c", e=EXPERTS),
                        onehot[rows, u, :, b, :].rearrange("p t (e c) -> p t e c", e=EXPERTS).bitcast(F32),
                        prob[rows, bass.ds(2 * n, 2), :].unsqueeze(3).to_broadcast([SEQ, 2, EXPERTS, CAP]),
                        ALU.mult).then_inc(s_cb, 1)
                    pool.wait_ge(s_cb, 2 * n + b + 1)

            steps(pool, UNITS, [(0, weigh_onehot)])
            with pool.Fori(1, EXPERTS // 2) as half:
                split_weights(half, 0)
                split_weights(half, 1)

        @block.scalar
        def _(act):
            s = nc.scalar
            act.wait_ge(s_early, 16)

            def project_copies(half, u):
                m = 2 * half + u
                act.wait_ge(s_kp, m + 1)
                s.activation(k_all[:, bass.ds(m * MT, MT)], ps[:, 6, :], ACT.Identity,
                             bias=bk_sb).then_inc(s_k, 1)
                act.wait_ge(s_xnt, m + 1)
                used(act, s_qp, m - 1)
                s.copy(xnt_ring[:, u, :], ps[:, 4, :]).then_inc(s_xntc, 1)
                act.wait_ge(s_vp, m + 1)
                s.copy(v_all[:, bass.ds(4 * m, 4), :], ps[:, 7, :].rearrange("p (t d) -> p t d", t=4)
                       ).then_inc(s_v, 1)

            def q_copy(half, u):
                m = 2 * half + u
                act.wait_ge(s_qp, m + 1)
                s.activation(q_all[:, bass.ds(m * MT, MT)], ps[:, 5, :], ACT.Identity,
                             bias=bq_sb).then_inc(s_q, 1)

            def project_slot(t):
                if t < MACROS:
                    project_copies(t // 2, t % 2)
                if 1 <= t <= MACROS:
                    q_copy((t - 1) // 2, (t - 1) % 2)

            for t in range(LED):
                project_slot(t)

            def spread_q(half, u):
                n = 2 * half + u
                if isinstance(n, int) and n == 0:
                    act.wait_ge(s_zero, 2)
                if isinstance(n, int) and n % 4 == 0:
                    act.wait_ge(s_q, 1 if n == 0 else MACROS)
                used(act, s_sc, n - 1)
                for g in range(GROUPS):
                    rows = slice(g * SEQ, (g + 1) * SEQ)
                    ins = s.copy(q_diag[rows, u, :, g * SEQ:(g + 1) * SEQ],
                                 q_all[rows, bass.ds(n * P, P)].rearrange("p (b q) -> p b q", b=2))
                ins.then_inc(s_qd, 1)

            def spread_v(half, u):
                n = 2 * half + u
                if isinstance(n, int) and n % 4 == 0:
                    act.wait_ge(s_v, 1 if n == 0 else MACROS)
                used(act, s_av, n - 1)
                for b in range(2):
                    src = v_all[b * SEQ:(b + 1) * SEQ, bass.ds(n, 1), :].rearrange(
                        "p o (g c h d) -> p (o g) c h d", g=2 * GROUPS, c=2, h=2)
                    for h in range(2):
                        to = v_diag[h * SEQ:(h + 1) * SEQ, u, b, :, :, :].rearrange("p g c n -> p (g c n)")
                        to = to.rearrange("p (g x) -> p g x", x=64)
                        first = HEAD * h
                        for c in range(2):
                            ins = s.copy(to[:, :, 48 * c + first:48 * c + first + HEAD], src[:, :, c, h, :])
                ins.then_inc(s_vd, 1)

            def exponential(half, u):
                n = 2 * half + u
                act.wait_ge(s_sub, n + 1)
                s.activation(probs[:, u, :], probs[:, u, :], ACT.Exp, scale=HEAD ** -0.5).then_inc(s_exp, 1)

            def probs_copy(half, u):
                n = 2 * half + u
                act.wait_ge(s_pt, n + 1)
                used(act, s_av, n - 1)
                s.copy(probs_t[:, u, :].rearrange("p (b n) -> p b n", b=2), ps[:, 4:6, :]).then_inc(s_ptc, 1)

            def o_copy(half, u):
                n = 2 * half + u
                act.wait_ge(s_av, n + 1)
                used(act, s_pj, n - 1)
                s.copy(ot_ring[:, u, :], ps[:, 6 + u, 0:P]).then_inc(s_otc, 1)

            def h_turn_copy(half, u):
                m = 2 * half + u
                act.wait_ge(s_htp, m + 1)
                used(act, s_lgp, m - 1)
                s.copy(ht_ring[:, u, :], ps[:, u, :]).then_inc(s_ht, 1)

            def h_high(half, u):
                m = 2 * half + u
                act.wait_ge(s_h, 4 * (m + 1))
                s.copy(h_hi[:, bass.ds(4 * m, 4), :], h_all[:, bass.ds(4 * m, 4), :]).then_inc(s_hhi, 1)

            def logits_copy(half, u):
                m = 2 * half + u
                act.wait_ge(s_lgp, m + 1)
                s.copy(logits[:, bass.ds(4 * m, 4), :],
                       ps[:, 2 + u, 0:4 * EXPERTS].rearrange("p (t e) -> p t e", t=4)).then_inc(s_lg, 1)

            def ln2_slot(i):
                if i == 0:
                    act.wait_ge(s_kd, TILES)
                for lag, stage in ((4, logits_copy), (2, h_turn_copy), (1, h_high)):
                    if 0 <= i - lag < MACROS:
                        stage((i - lag) // 2, (i - lag) % 2)

            steps(act, TILES, [(4, probs_copy), (2, exponential), (5, o_copy), (0, spread_q), (3, spread_v)],
                  lead=lambda t: project_slot(LED + t - 1) if t else None, drain=ln2_slot)

            def route_exp(half):
                tiles = slice(half * TILES // 2, (half + 1) * TILES // 2)
                act.wait_ge(s_rsh, half + 1)
                s.activation(rt[1][:, tiles, :], rt[0][:, tiles, :], ACT.Exp).then_inc(s_rexp, 1)

            for i in range(5, MACROS + 4):
                ln2_slot(i)
                if i == MACROS:
                    route_exp(0)
            route_exp(1)

            def slots_copy(t):
                def copy(half, u):
                    n = 2 * half + u
                    act.wait_ge(s_g[t], n + 1)
                    s.copy(slots_at(slots_hi, 2 * n + t), ps[:, 4 * u + t, 0:2 * SLOTS]).then_inc(s_gc[t], 1)
                return copy

            def comb_copy(half, u):
                n = 2 * half + u
                act.wait_ge(s_ctp, n + 1)
                s.copy(comb_t[0:HALF, :, bass.ds(n * 2 * P, 2 * P)].rearrange("p h (t n) -> p h t n", t=2),
                       ps[0:HALF, 4 * u:4 * u + 4, 3 * P:4 * P].rearrange("p (h t) n -> p h t n", h=2)
                       ).then_inc(s_ctc, 1)

            steps(act, UNITS, [(0, slots_copy(0)), (1, comb_copy), (0, slots_copy(1))])

            def high_part(tile, part, c):
                rows = UPPER if c == LAST else slice(0, P)
                act.wait_ge(s_gt, tile * CHUNKS + c + 1)
                if c == 0:
                    used(act, s_dn, tile - 1)
                s.copy(gated_hi[rows, part % 2, c, :], gated[rows, c % 2, :]).then_inc(s_ghi, 1)

            def expert(half, u):
                for part in range(PARTS):
                    tile = (2 * half + u) * PARTS + part
                    for c in range(CHUNKS):
                        q = tile * CHUNKS + c
                        act.wait_ge(s_h1, q + 1)
                        used(act, s_gt, q - 1)
                        if c == LAST:
                            s.activation(silu[UPPER, c % 2, :], ps[LOWER, BOTH, 0:PS], ACT.Silu).then_inc(s_si, 1)
                        else:
                            s.activation(silu[:, c % 2, :], ps[:, UP[0] + c, 0:PS], ACT.Silu).then_inc(s_si, 1)
                        if c > 0:
                            high_part(tile, part, c - 1)
                        elif not isinstance(tile, int) or tile > 0:
                            high_part(tile - 1, (part - 1) % PARTS, LAST)

            expert(0, 0)
            expert(0, 1)
            with act.Fori(1, EXPERTS // 2) as half:
                expert(half, 0)
                expert(half, 1)
            high_part(EXPERTS * PARTS - 1, PARTS - 1, LAST)

            def slot_copy(half, u):
                m = 2 * half + u
                for bank in range(0, 4, 2):
                    act.wait_ge(s_st[bank], m + 1)
                    used(act, s_cm, m - 1)
                    s.copy(slot_rows[0:HALF, u, 4 * bank:4 * bank + 4, :],
                           ps[0:HALF, bank, :].rearrange("p (n d) -> p n d", n=4)).then_inc(s_sr[bank], 1)

            steps(act, MACROS, [(0, slot_copy)])

        @block.vector
        def _(dve):
            v = nc.vector

            def norm_stats(src, n, u, bn, mv):
                for t in range(4):
                    v.bn_stats(stats[:, u, t, :], src[:, bass.ds(4 * n + t, 1), :].rearrange("p t d -> p (t d)")
                               ).then_inc(bn, 1)
                dve.wait_ge(bn, 4 * (n + 1))
                apart(dve)
                for t in range(4):
                    v.bn_aggr(meanvar[:, u, t, :], stats[:, u, t, :]).then_inc(mv, 1)

            def ln1_stats(m):
                u = m % 2
                dve.wait_ge(s_x[m], 16)
                norm_stats(x_all, m, u, s_bn, s_mv)

            def ln1_apply(half, u):
                m = 2 * half + u
                dve.wait_ge(s_rstd, m + 1)
                used(dve, s_xnt, m - 1)
                for t in range(4):
                    v.tensor_scalar(xn_ring[:, u, t, :].unsqueeze(1), x_all[:, bass.ds(4 * m + t, 1), :],
                                    meanvar[:, u, t, 0:1], rstd[:, u, t:t + 1],
                                    ALU.subtract, ALU.mult).then_inc(s_xn, 1)

            for m in range(MACROS + 1):
                if m < MACROS:
                    used(dve, s_xn, 4 * (m - 1))
                    ln1_stats(m)
                if m == 0:
                    dve.wait_ge(s_late, 16)
                    v.tensor_scalar(bv_rows[:, :], cv["tri"], 0.0, bv_sb, ALU.mult, ALU.add).then_inc(s_bvr, 1)
                if m == 1:
                    dve.wait_ge(s_bop, 1)
                    v.tensor_tensor(bo_sb, ps[:, 0, 0:D], bo_sb, ALU.add).then_inc(s_bo, 1)
                if m >= 1:
                    ln1_apply((m - 1) // 2, (m - 1) % 2)

            NB = 2 * GH

            def head_scores(u):
                return ps[:, 2 * u:2 * u + 2, :].rearrange("p b (h k) -> p (b h) k", k=SEQ)

            def maximum(half, u):
                n = 2 * half + u
                dve.wait_ge(s_sc, n + 1)
                v.tensor_reduce(row_max[:, u, :], head_scores(u), X, ALU.max).then_inc(s_mx, 1)

            def shift(half, u):
                n = 2 * half + u
                dve.wait_ge(s_mx, n + 1)
                used(dve, s_pt, n - 1)
                v.tensor_tensor(probs[:, u, :].rearrange("p (n k) -> p n k", k=SEQ), head_scores(u),
                                row_max[:, u, :].unsqueeze(2).to_broadcast([P, NB, SEQ]),
                                ALU.subtract).then_inc(s_sub, 1)

            def row_sums(half, u):
                n = 2 * half + u
                dve.wait_ge(s_exp, n + 1)
                v.tensor_reduce(row_sum[:, u, :], probs[:, u, :].rearrange("p (n k) -> p n k", k=SEQ), X,
                                ALU.add).then_inc(s_sum, 1)

            def denominator(half, u):
                n = 2 * half + u
                dve.wait_ge(s_sum, n + 1)
                used(dve, s_pn, n - 1)
                v.reciprocal(rden[:, u, :], row_sum[:, u, :]).then_inc(s_rd, 1)

            def add_residual(half, u):
                n = 2 * half + u
                if isinstance(n, int) and n == 0:
                    dve.wait_ge(s_xb, MACROS)
                dve.wait_ge(s_pj, n + 1)
                v.tensor_tensor(x1_all[:, bass.ds(n, 1), :], ps[:, 6 + u, P:P + D].unsqueeze(1),
                                x1_all[:, bass.ds(n, 1), :], ALU.add).then_inc(s_x1, 1)

            def ln2_stats(half, u):
                n = 2 * half + u
                dve.wait_ge(s_x1, n + 1)
                used(dve, s_mvt, n - 1)
                apart(dve)
                v.bn_stats(stats[:, u, 0, :], x1_all[:, bass.ds(n, 1), :].rearrange("p t d -> p (t d)")
                           ).then_inc(s_bn2, 1)

            def ln2_meanvar(half, u):
                n = 2 * half + u
                dve.wait_ge(s_bn2, n + 1)
                used(dve, s_mv2, n - 1)
                apart(dve)
                v.bn_aggr(meanvar[:, u, 0, :], stats[:, u, 0, :]).then_inc(s_mvt, 1)

            def ln2_apply(half, u):
                m = 2 * half + u
                if m == 0:
                    dve.wait_ge(s_qd, TILES)
                dve.wait_ge(s_rstd2, m + 1)
                for t in range(4):
                    tile = bass.ds(4 * m + t, 1)
                    v.tensor_scalar(h_all[:, tile, :], x1_all[:, tile, :],
                                    meanvar2[:, tile, 0], rstd2[:, tile],
                                    ALU.subtract, ALU.mult).then_inc(s_h, 1)

            def h_low(half, u):
                m = 2 * half + u
                dve.wait_ge(s_hhi, m + 1)
                v.tensor_tensor(h_lo[:, bass.ds(4 * m, 4), :], h_all[:, bass.ds(4 * m, 4), :],
                                h_hi[:, bass.ds(4 * m, 4), :].bitcast(F32), ALU.subtract).then_inc(s_hlo, 1)

            def ln2_slot(m):
                if m < MACROS:
                    ln2_apply(m // 2, m % 2)
                if m >= 2:
                    h_low((m - 2) // 2, m % 2)

            steps(dve, TILES, [(5, add_residual), (0, maximum), (1, row_sums), (6, ln2_stats), (1, denominator),
                               (0, shift), (7, ln2_meanvar)], drain=ln2_slot)

            done = [0]

            def then(ins):
                done[0] += 1
                ins.then_inc(s_rt, 1)
                dve.wait_ge(s_rt, done[0])

            HT = TILES // 2
            rank = cv["rank"].unsqueeze(1).to_broadcast([P, HT, EXPERTS])

            def part(a, half):
                return a[:, half * HT:(half + 1) * HT, :]

            def scalars(i, half):
                return rs[i][:, half * HT:(half + 1) * HT]

            def wide(i, half):
                return scalars(i, half).unsqueeze(2).to_broadcast([P, HT, EXPERTS])

            def route_shift(half):
                dve.wait_ge(s_lg, MACROS // 2 * (half + 1))
                then(v.tensor_reduce(scalars(0, half), part(logits, half), X, ALU.max))
                v.tensor_tensor(part(rt[0], half), part(logits, half), wide(0, half), ALU.subtract).then_inc(s_rsh, 1)

            def first_largest(half, values, largest, equal, weighted, best, chosen):
                then(v.tensor_reduce(scalars(largest, half), part(values, half), X, ALU.max))
                then(v.tensor_tensor(part(equal, half), part(values, half), wide(largest, half), ALU.is_equal))
                then(v.tensor_tensor(part(weighted, half), part(equal, half), rank, ALU.mult))
                then(v.tensor_reduce(scalars(best, half), part(weighted, half), X, ALU.max))
                then(v.tensor_tensor(part(chosen, half), part(weighted, half), wide(best, half), ALU.is_equal))

            def route_choose(half):
                dve.wait_ge(s_rexp, half + 1)
                then(v.tensor_reduce(scalars(1, half), part(rt[1], half), X, ALU.add))
                then(v.reciprocal(scalars(2, half), scalars(1, half)))
                then(v.tensor_tensor(part(prob, half), part(rt[1], half), wide(2, half), ALU.mult))
                first_largest(half, prob, 3, rt[2], rt[3], 4, rt[4])
                then(v.scalar_tensor_tensor(out=part(rt[5], half), in0=part(rt[4], half), scalar=-2.0,
                                            in1=part(prob, half), op0=ALU.mult, op1=ALU.add))
                first_largest(half, rt[5], 5, rt[2], rt[3], 0, rt[6])
                v.tensor_tensor(part(rt[7], half), part(rt[4], half), part(rt[6], half), ALU.add).then_inc(s_ch, 1)

            def route_places(half):
                cols = slice(half * HT * EXPERTS, (half + 1) * HT * EXPERTS)
                dve.wait_ge(s_pos, half + 1)
                v.tensor_tensor(part(places, half), ps[:, 6 + half, cols].rearrange("p (t e) -> p t e", e=EXPERTS),
                                part(rt[7], half), ALU.mult).then_inc(s_pl, 1)

            ln2_slot(7)
            route_shift(0)
            ln2_slot(8)
            route_choose(0)
            route_shift(1)
            ln2_slot(9)
            route_places(0)
            route_choose(1)
            route_places(1)
            dve.wait_ge(s_pl, 2)

            def one_hot(half, u):
                n = 2 * half + u
                if isinstance(n, int) and n == 0:
                    dve.wait_ge(s_zero, 3)
                used(dve, s_cb, 2 * (n - 1))
                used(dve, s_g[2], n - 1)
                used(dve, s_g[3], n - 1)
                for b in range(2):
                    rows = slice(b * SEQ, (b + 1) * SEQ)
                    ins = v.tensor_tensor(
                        onehot[rows, u, :, b, :].rearrange("p t (e c) -> p t e c", e=EXPERTS),
                        places[rows, bass.ds(2 * n, 2), :].unsqueeze(3).to_broadcast([SEQ, 2, EXPERTS, CAP]),
                        cv["place"][rows, :].unsqueeze(1).unsqueeze(1).to_broadcast([SEQ, 2, EXPERTS, CAP]),
                        ALU.is_equal)
                ins.then_inc(s_oh, 1)

            def slots_copy(half, u):
                n = 2 * half + u
                for t in range(2):
                    dve.wait_ge(s_g[2 + t], n + 1)
                    v.tensor_copy(slots_at(slots_lo, 2 * n + t), ps[:, 4 * u + 2 + t, 0:2 * SLOTS]
                                  ).then_inc(s_gc[2 + t], 1)

            steps(dve, UNITS, [(0, one_hot), (1, slots_copy)])

            def expert_out_copy(tile, e, part):
                dve.wait_ge(s_dn, tile + 1)
                v.tensor_copy(expert_slots(expert_out, e, part),
                              ps[:, DOWN, 0:PS].rearrange("p (b c) -> p b c", c=CAP)).then_inc(s_eo, 1)

            def low_part(tile, part, c):
                dve.wait_ge(s_ghi, tile * CHUNKS + c + 1)
                if c == 0:
                    used(dve, s_dn, tile - 1)
                rows, low = (UPPER, gated_hi[LOWER, part % 2, c, :]) if c == LAST else \
                    (slice(0, P), gated_lo[:, part % 2, c, :])
                v.tensor_tensor(low, gated[rows, c % 2, :], gated_hi[rows, part % 2, c, :].bitcast(F32),
                                ALU.subtract).then_inc(s_glo, 1)

            def expert(half, u):
                e = 2 * half + u
                for part in range(PARTS):
                    tile = e * PARTS + part
                    for c in range(CHUNKS):
                        q = tile * CHUNKS + c
                        if c < LAST:
                            dve.wait_ge(s_h3, tile * LAST + c + 1)
                        dve.wait_ge(s_si, q + 1)
                        used(dve, s_ghi, q - 1)
                        used(dve, s_glo, q - 1)
                        rows, bank = (UPPER, BOTH) if c == LAST else (slice(0, P), UP[1] + c)
                        v.tensor_tensor(gated[rows, c % 2, :], ps[rows, bank, 0:PS], silu[rows, c % 2, :],
                                        ALU.mult).then_inc(s_gt, 1)
                        if c > 0:
                            low_part(tile, part, c - 1)
                        elif not isinstance(tile, int) or tile > 0:
                            low_part(tile - 1, (part - 1) % PARTS, LAST)
                    if not isinstance(tile, int) or tile > 0:
                        expert_out_copy(tile - 1, e if part else e - 1, (part - 1) % PARTS)

            for i in range(4):
                dve.wait_ge(s_g[i], UNITS)
            expert(0, 0)
            expert(0, 1)
            with dve.Fori(1, EXPERTS // 2) as half:
                expert(half, 0)
                expert(half, 1)
            low_part(EXPERTS * PARTS - 1, PARTS - 1, LAST)
            expert_out_copy(EXPERTS * PARTS - 1, EXPERTS - 1, PARTS - 1)

            def slot_copy(half, u):
                m = 2 * half + u
                for bank in range(1, 4, 2):
                    dve.wait_ge(s_st[bank], m + 1)
                    used(dve, s_cm, m - 1)
                    v.tensor_copy(slot_rows[0:HALF, u, 4 * bank:4 * bank + 4, :],
                                  ps[0:HALF, bank, :].rearrange("p (n d) -> p n d", n=4)).then_inc(s_sr[bank], 1)

            def add_experts(half, u):
                m = 2 * half + u
                dve.wait_ge(s_cm, m + 1)
                used(dve, s_os[u], 16 * half)
                v.tensor_tensor(out_ring[:, u, :, :], ps[:, 4 + u, :].rearrange("p (t d) -> p t d", t=4),
                                x1_all[:, bass.ds(4 * m, 4), :], ALU.add).then_inc(s_oc, 1)

            steps(dve, MACROS, [(0, slot_copy), (1, add_experts)])

        @block.tensor
        def _(pe):
            mm = nc.tensor.matmul
            turn = nc.tensor.transpose
            pe.wait_ge(s_early, 16)

            def project(half, u):
                m = 2 * half + u
                pe.wait_ge(s_ctx[u], 16 * (half + 1))
                used(pe, s_k, m)
                mm(ps[:, 6, :], wk_sb, ctx_ring[:, u, :], start=True, stop=True).then_inc(s_kp, 1)
                used(pe, s_v, m)
                for t in range(4):
                    ins = mm(ps[:, 7, t * D:(t + 1) * D], ctx_ring[:, u, t * P:(t + 1) * P], wv_sb,
                             start=True, stop=True)
                ins.then_inc(s_vp, 1)
                if isinstance(m, int) and m == 0:
                    pe.wait_ge(s_bvr, 1)
                    mm(ps[:, 0, 0:D], bv_rows[:, :], wo_sb, start=True, stop=True).then_inc(s_bop, 1)
                pe.wait_ge(s_xn, 4 * (m + 1))
                used(pe, s_xntc, m)
                for t in range(4):
                    ins = turn(ps[:, 4, t * P:(t + 1) * P], xn_ring[:, u, t, :], ident)
                ins.then_inc(s_xnt, 1)

            def project_q(half, u):
                m = 2 * half + u
                pe.wait_ge(s_xntc, m + 1)
                used(pe, s_q, m)
                mm(ps[:, 5, :], wq_sb, xnt_ring[:, u, :], start=True, stop=True).then_inc(s_qp, 1)

            def project_slot(t):
                if t < MACROS:
                    project(t // 2, t % 2)
                if 1 <= t <= MACROS:
                    project_q((t - 1) // 2, (t - 1) % 2)

            for t in range(LED):
                project_slot(t)

            def scores(half, u):
                n = 2 * half + u
                if isinstance(n, int) and n == 0:
                    pe.wait_ge(s_bo, 1)
                pe.wait_ge(s_qd, n + 1)
                pe.wait_ge(s_kd, n + 1)
                used(pe, s_sub, n - 1)
                for b in range(2):
                    ins = mm(ps[:, 2 * u + b, :], q_diag[:, u, b, :], k_diag[:, u, b, :, :], start=True, stop=True)
                ins.then_inc(s_sc, 1)

            def turn_probs(half, u):
                n = 2 * half + u
                if isinstance(n, int) and n == 0:
                    pe.wait_ge(s_xntc, MACROS)
                    pe.wait_ge(s_q, MACROS)
                pe.wait_ge(s_pn, n + 1)
                used(pe, s_ptc, n)
                for i in range(2 * PAIRS):
                    ins = turn(ps[:, 4 + i // 4, (i % 4) * P:(i % 4 + 1) * P], probs[:, u, i * P:(i + 1) * P], ident)
                ins.then_inc(s_pt, 1)

            def weigh(half, u):
                n = 2 * half + u
                if isinstance(n, int) and n == 0:
                    pe.wait_ge(s_k, MACROS)
                    pe.wait_ge(s_v, MACROS)
                pe.wait_ge(s_vd, n + 1)
                pe.wait_ge(s_ptc, n + 1)
                used(pe, s_x1, n - 1)
                for b in range(2):
                    for g in range(GROUPS):
                        for c in range(PAIRS):
                            rows = 32 * (2 * g + c // 2)
                            src = (b * PAIRS + c) * P + g * SEQ
                            ins = mm(ps[rows:rows + 32, 6 + u, b * SEQ:(b + 1) * SEQ], v_diag[:, u, b, g, c, :],
                                     probs_t[:, u, src:src + SEQ], start=(c % 2 == 0), stop=(c % 2 == 1))
                ins.then_inc(s_av, 1)

            def out_product(half, u):
                n = 2 * half + u
                pe.wait_ge(s_otc, n + 1)
                mm(ps[:, 6 + u, P:P + D], ot_ring[:, u, :], wo_sb, start=True, stop=True).then_inc(s_pj, 1)


            def h_turn(m):
                if m == 0:
                    pe.wait_ge(s_sub, TILES)
                pe.wait_ge(s_h, 4 * (m + 1))
                used(pe, s_ht, m - 1)
                for t in range(4):
                    ins = turn(ps[:, m % 2, t * P:(t + 1) * P], h_all[:, 4 * m + t, :], ident)
                ins.then_inc(s_htp, 1)

            def route(m):
                pe.wait_ge(s_ht, m + 1)
                used(pe, s_lg, m - 1)
                for t in range(4):
                    ins = mm(ps[:, 2 + m % 2, t * EXPERTS:(t + 1) * EXPERTS], ht_ring[:, m % 2, t * P:(t + 1) * P],
                             gate_sb, start=True, stop=True)
                ins.then_inc(s_lgp, 1)

            def ln2_slot(m):
                if m < MACROS:
                    h_turn(m)
                if m >= 2:
                    route(m - 2)

            steps(pe, TILES, [(0, scores), (3, weigh), (4, out_product), (2, turn_probs)],
                  lead=lambda t: project_slot(LED + t), drain=ln2_slot)
            for m in range(4, MACROS + 2):
                ln2_slot(m)

            for half in range(2):
                tiles = slice(half * TILES // 2, (half + 1) * TILES // 2)
                cols = slice(tiles.start * EXPERTS, tiles.stop * EXPERTS)
                pe.wait_ge(s_ch, half + 1)
                mm(ps[:, 6 + half, cols], cv["tri"], rt[7][:, tiles, :], start=True, stop=True).then_inc(s_pos, 1)

            def gather(n, lo):
                u = n % 2
                if lo == 0:
                    pe.wait_ge(s_oh, n + 1)
                if n == 0:
                    pe.wait_ge(s_hlo if lo else s_hhi, MACROS)
                part = h_lo if lo else h_hi
                for t in range(2):
                    used(pe, s_gc[2 * lo + t], n - 1)
                if lo == 0:
                    used(pe, s_ctc, n - 1)
                for t in range(2):
                    mm(ps[:, 4 * u + 2 * lo + t, 0:2 * SLOTS], part[:, 2 * n + t, :], onehot[:, u, t, :, :],
                       start=True, stop=True).then_inc(s_g[2 * lo + t], 1)

            def turn_comb(n):
                u = n % 2
                pe.wait_ge(s_cb, 2 * (n + 1))
                for i in range(4):
                    pe.wait_ge(s_gc[i], n + 1)
                for h in range(2):
                    for t in range(2):
                        ins = turn(ps[0:HALF, 4 * u + 2 * h + t, 3 * P:4 * P],
                                   comb[:, u, t, h * HALF:(h + 1) * HALF], ident)
                ins.then_inc(s_ctp, 1)

            for n in range(UNITS + 1):
                if n < UNITS:
                    gather(n, 0)
                if n >= 1:
                    turn_comb(n - 1)
                if n < UNITS:
                    gather(n, 1)

            def up(tile, e, part, u):
                hi, lo = expert_slots(slots_hi, e, part), expert_slots(slots_lo, e, part)

                def products(bank, first, done):
                    to, cols = ps[:, bank, 0:PS], slice(first, first + P)
                    mm(to, w13_lo[:, u, cols], hi, start=True, stop=False)
                    mm(to, w13_hi[:, u, cols], lo, start=False, stop=False)
                    mm(to, w13_hi[:, u, cols], hi, start=False, stop=True).then_inc(done, 1)

                for c in range(LAST):
                    used(pe, s_si, (tile - 1) * CHUNKS + c + 1)
                    products(UP[0] + c, c * P, s_h1)
                    used(pe, s_gt, (tile - 1) * CHUNKS + c + 1)
                    products(UP[1] + c, (LAST + c) * P, s_h3)
                used(pe, s_gt, tile * CHUNKS)
                products(BOTH, 2 * LAST * P, s_h1)

            def down(tile, part, u):
                used(pe, s_eo, tile)
                bank, u2 = ps[:, DOWN, 0:PS], part % 2
                for c in range(LAST):
                    pe.wait_ge(s_ghi, tile * CHUNKS + c + 1)
                    mm(bank, w2_lo[:, u, c, :], gated_hi[:, u2, c, :], start=(c == 0), stop=False)
                    mm(bank, w2_hi[:, u, c, :], gated_hi[:, u2, c, :], start=False, stop=False)
                    pe.wait_ge(s_glo, tile * CHUNKS + c + 1)
                    mm(bank, w2_hi[:, u, c, :], gated_lo[:, u2, c, :], start=False, stop=False)
                pe.wait_ge(s_ghi, (tile + 1) * CHUNKS)
                mm(bank, w2_lo[UPPER, u, LAST, :], gated_hi[UPPER, u2, LAST, :], start=False, stop=False)
                pe.wait_ge(s_glo, (tile + 1) * CHUNKS)
                mm(bank, w2_hi[:, u, LAST, :], gated_hi[:, u2, LAST, :], start=False, stop=True).then_inc(s_dn, 1)

            def expert(half, u):
                e = 2 * half + u
                pe.wait_ge(s_wlo, 2 * (e + 1))
                for part in range(PARTS):
                    tile = e * PARTS + part
                    up(tile, e, part, u)
                    if not isinstance(tile, int) or tile > 0:
                        down(tile - 1, (part - 1) % PARTS, u if part else 1 - u)

            pe.wait_ge(s_ctc, UNITS)
            for i in range(4):
                pe.wait_ge(s_gc[i], UNITS)
            expert(0, 0)
            expert(0, 1)
            with pe.Fori(1, EXPERTS // 2) as half:
                expert(half, 0)
                expert(half, 1)
            down(EXPERTS * PARTS - 1, PARTS - 1, 1)

            def turn_slots(m):
                for bank in range(4):
                    used(pe, s_sr[bank], m)
                    for i in range(4):
                        at = (16 * m + 4 * bank + i) * HALF
                        ins = turn(ps[0:HALF, bank, i * D:(i + 1) * D], expert_out[:, at:at + HALF], ident)
                    ins.then_inc(s_st[bank], 1)

            def combine(m):
                used(pe, s_oc, m - 1)
                for b in range(8):
                    if b % 2 == 0:
                        pe.wait_ge(s_sr[b // 2], m + 1)
                    rows = slice(b % 2 * SEQ, (b % 2 + 1) * SEQ)
                    for h in range(2):
                        ins = mm(ps[rows, 4 + m % 2, b // 2 * D:(b // 2 + 1) * D],
                                 comb_t[0:HALF, h, m * MT + b * SEQ:m * MT + (b + 1) * SEQ],
                                 slot_rows[0:HALF, m % 2, 2 * b + h, :], start=(h == 0), stop=(h == 1))
                ins.then_inc(s_cm, 1)

            pe.wait_ge(s_eo, EXPERTS * PARTS)
            for m in range(MACROS + 1):
                if m < MACROS:
                    turn_slots(m)
                if m >= 1:
                    combine(m - 1)


def kernel(**inputs):
    import numpy as _np
    import concourse.bacc as _bacc
    from concourse import mybir as _mybir
    from concourse.bass_utils import run_bass_kernel_spmd as _run

    def laid(name):
        return _np.asarray(inputs[name])

    small = dict(constants(), gate=laid("L0_ffn_gate_w").T,
                 bo=_np.broadcast_to(laid("L0_xattn_bo"), (P, D)))
    for n in "qkvo":
        small[f"w{n}"] = laid(f"L0_xattn_W{n}").T
    for n in "qkv":
        small[f"b{n}"] = laid(f"L0_xattn_b{n}").reshape(-1, 1)

    def packed(columns):
        return _np.ascontiguousarray(_np.concatenate([small[n] for n in columns], axis=1))

    arrays = {
        "x": laid("x").reshape(TOKENS, D),
        "ctx_t": _np.ascontiguousarray(laid("ctx_1024").reshape(TOKENS, D).T),
        "early": packed(EARLY),
        "late": packed(LATE),
        "w13": _np.ascontiguousarray(_np.concatenate(
            [laid(n)[:, :, at:to] for at, to in ((0, LAST * P), (LAST * P, FFN)) for n in ("L0_ffn_w1", "L0_ffn_w3")],
            axis=2).transpose(1, 0, 2).reshape(D, EXPERTS * 2 * FFN)),
        "w2": _np.ascontiguousarray(_np.concatenate([laid("L0_ffn_w2"), laid("L0_ffn_w2")[:, LAST * P:, :]], axis=1)
                                    .reshape(EXPERTS * CHUNKS, P, D).transpose(1, 0, 2)),
    }
    nc = _bacc.Bacc("TRN2", target_bir_lowering=False, num_devices=1)
    args = [nc.dram_tensor(f"in_{n}", a.shape, _mybir.dt.from_np(a.dtype), kind="ExternalInput").ap()
            for n, a in arrays.items()]
    out = nc.dram_tensor("out", (TOKENS, D), _mybir.dt.float32, kind="ExternalOutput").ap()
    build(nc, *args, out)
    r = _run(nc, [{f"in_{n}": a for n, a in arrays.items()}], core_ids=[0])
    return r.results[0]["out"].reshape(SEQS, SEQ, D)
```
